# Optimizing a Trainium2 kernel written in Bass

```python
import numpy as np
import jax
import jax.numpy as jnp

def _softmax(x, axis=-1):
    return jax.nn.softmax(x, axis=axis)

def _gelu(x):
    return jax.nn.gelu(x, approximate=True)

def _silu(x):
    return jax.nn.silu(x)

def _sigmoid(x):
    return jax.nn.sigmoid(x)

def _layernorm(x, axis=-1, eps=1e-05):
    m = jnp.mean(x, axis=axis, keepdims=True)
    v = jnp.var(x, axis=axis, keepdims=True)
    return (x - m) / jnp.sqrt(v + eps)

def _scatter_add(tgt, idx, src, axis=0):
    return tgt.at[idx].add(src)

def _segment_sum(src, seg, n):
    return jax.ops.segment_sum(src, seg, n)
kernel_name = 'mk_adaln_d1_jaxref_r8_930825'

def setup_inputs(seed: int=0):
    np.random.seed(seed)
    _w = jnp.asarray

    def _L0_attn_setup():
        import jax, jax.numpy as jnp
        import numpy as np
        HIDDEN = 512
        NUM_HEADS = 32
        HEAD_DIM = HIDDEN // NUM_HEADS

        def _fp8_roundtrip(x):
            return x.astype(jnp.float8_e4m3fn).astype(jnp.float32)
        key = jax.random.key(seed)
        ks = jax.random.split(key, 10)
        B, S = (2, 512)
        hidden_states = jax.random.normal(ks[0], (B, S, HIDDEN), dtype=jnp.float32)
        scale = 0.02

        def lin(kw, kb):
            w = jax.random.normal(kw, (HIDDEN, HIDDEN), dtype=jnp.float32) * scale
            b = jax.random.normal(kb, (HIDDEN,), dtype=jnp.float32) * scale
            return (w, b)
        wq, bq = lin(ks[1], ks[2])
        wk, bk = lin(ks[3], ks[4])
        wv, bv = lin(ks[5], ks[6])
        wl, bl = lin(ks[7], ks[8])
        wq, bq = (_fp8_roundtrip(wq), _fp8_roundtrip(bq))
        wk, bk = (_fp8_roundtrip(wk), _fp8_roundtrip(bk))
        wv, bv = (_fp8_roundtrip(wv), _fp8_roundtrip(bv))
        return {'hidden_states': hidden_states, 'wq': wq, 'bq': bq, 'wk': wk, 'bk': bk, 'wv': wv, 'bv': bv, 'wl': wl, 'bl': bl}
    _L0_attn_in = _L0_attn_setup()

    def _L0_ffn_setup():
        import jax, jax.numpy as jnp
        import numpy as np
        B, T, D_IN, D_OUT = (8, 256, 512, 512)
        N_LORAS, RANK = (16, 32)
        SCALING = 1.0
        key = jax.random.key(seed)
        ks = jax.random.split(key, 8)
        std = 1.0 / D_IN ** 0.5
        x = jax.random.normal(ks[0], (B, T, D_IN), dtype=jnp.float32)
        idx = jax.random.randint(ks[1], (B,), 0, N_LORAS)
        gate = jax.nn.one_hot(idx, N_LORAS, dtype=jnp.float32)
        kernel = jax.random.normal(ks[2], (D_IN, D_OUT), dtype=jnp.float32) * std
        bias = jnp.zeros((D_OUT,), dtype=jnp.float32)
        lora_A = jax.random.normal(ks[3], (N_LORAS, RANK, D_IN), dtype=jnp.float32) * std
        lora_B = jax.random.normal(ks[4], (N_LORAS, D_OUT, RANK), dtype=jnp.float32) * 0.01
        lora_A_shared = jax.random.normal(ks[5], (RANK, D_IN), dtype=jnp.float32) * std
        lora_B_shared = jax.random.normal(ks[6], (D_OUT, RANK), dtype=jnp.float32) * 0.01
        return {'x': x, 'gate': gate, 'kernel': kernel, 'bias': bias, 'lora_A': lora_A, 'lora_B': lora_B, 'lora_A_shared': lora_A_shared, 'lora_B_shared': lora_B_shared}
    _L0_ffn_in = _L0_ffn_setup()
    _L0_c = _w((lambda *s: np.random.randn(*s).astype(np.float32) * 0.05)(1, 512))
    _L0_wmod = _w((lambda *s: np.random.randn(*s).astype(np.float32) * 0.05)(512, 6 * 512) * 512 ** (-0.5))
    _d = {'L0_attn_hidden_states': _L0_attn_in['hidden_states'], 'L0_attn_wq': _L0_attn_in['wq'], 'L0_attn_bq': _L0_attn_in['bq'], 'L0_attn_wk': _L0_attn_in['wk'], 'L0_attn_bk': _L0_attn_in['bk'], 'L0_attn_wv': _L0_attn_in['wv'], 'L0_attn_bv': _L0_attn_in['bv'], 'L0_attn_wl': _L0_attn_in['wl'], 'L0_attn_bl': _L0_attn_in['bl'], 'L0_ffn_gate': _L0_ffn_in['gate'], 'L0_ffn_kernel': _L0_ffn_in['kernel'], 'L0_ffn_bias': _L0_ffn_in['bias'], 'L0_ffn_lora_A': _L0_ffn_in['lora_A'], 'L0_ffn_lora_B': _L0_ffn_in['lora_B'], 'L0_ffn_lora_A_shared': _L0_ffn_in['lora_A_shared'], 'L0_ffn_lora_B_shared': _L0_ffn_in['lora_B_shared'], 'L0_c': _L0_c, 'L0_wmod': _L0_wmod}
    _x0 = _d['L0_attn_hidden_states']
    _d['L0_attn_hidden_states'] = jax.random.normal(jax.random.fold_in(jax.random.key(seed), 1), (1, 1024, 512), dtype=_x0.dtype)
    del _x0
    return _d

def reference(L0_attn_hidden_states, L0_attn_wq, L0_attn_bq, L0_attn_wk, L0_attn_bk, L0_attn_wv, L0_attn_bv, L0_attn_wl, L0_attn_bl, L0_ffn_gate, L0_ffn_kernel, L0_ffn_bias, L0_ffn_lora_A, L0_ffn_lora_B, L0_ffn_lora_A_shared, L0_ffn_lora_B_shared, L0_c, L0_wmod):

    def _L0_attn_ref(hidden_states, wq, bq, wk, bk, wv, bv, wl, bl):
        import jax, jax.numpy as jnp
        import numpy as np
        HIDDEN = 512
        NUM_HEADS = 32
        HEAD_DIM = HIDDEN // NUM_HEADS

        def _fp8_roundtrip(x):
            return x.astype(jnp.float8_e4m3fn).astype(jnp.float32)
        B, S, E = hidden_states.shape
        H, D = (NUM_HEADS, HEAD_DIM)
        q = (hidden_states @ wq.T + bq).reshape(B, S, H, D)
        k = (hidden_states @ wk.T + bk).reshape(B, S, H, D)
        v = (hidden_states @ wv.T + bv).reshape(B, S, H, D)
        latent = hidden_states @ wl.T + bl
        scores = jnp.einsum('bshd,bstd->bsht', q, k) / np.sqrt(D).astype(np.float32)
        probs = jax.nn.softmax(scores, axis=-1)
        context = jnp.einsum('bsht,bstd->bshd', probs, v).reshape(B, S, E)
        return context

    def _L0_ffn_ref(x, gate, kernel, bias, lora_A, lora_B, lora_A_shared, lora_B_shared):
        import jax, jax.numpy as jnp
        import numpy as np
        B, T, D_IN, D_OUT = (8, 256, 512, 512)
        N_LORAS, RANK = (16, 32)
        SCALING = 1.0
        base_out = jnp.matmul(x, kernel) + bias
        b = gate.shape[0]
        x_flat = x.reshape(b, -1, x.shape[-1])
        A_eff = jnp.einsum('bn,nri->bri', gate, lora_A)
        B_eff = jnp.einsum('bn,nor->bor', gate, lora_B)
        Ax = jnp.einsum('bri,bti->btr', A_eff, x_flat)
        delta_flat = jnp.einsum('bor,btr->bto', B_eff, Ax)
        Ax_s = jnp.einsum('ri,bti->btr', lora_A_shared, x_flat)
        delta_flat = delta_flat + jnp.einsum('or,btr->bto', lora_B_shared, Ax_s)
        delta = delta_flat.reshape(x.shape[:-1] + (kernel.shape[-1],))
        return base_out + (SCALING * delta).astype(base_out.dtype)
    x = L0_attn_hidden_states
    mod = (_silu(L0_c) @ L0_wmod).reshape(L0_c.shape[0], 6, 1, -1)
    sa, ca, ga, sb, cb, gb = (mod[:, 0], mod[:, 1], mod[:, 2], mod[:, 3], mod[:, 4], mod[:, 5])
    ga = (2 * (ga >= 0) - 1) * jnp.maximum(jnp.abs(ga), 0.25)
    gb = (2 * (gb >= 0) - 1) * jnp.maximum(jnp.abs(gb), 0.25)
    h = _layernorm(x, axis=-1) * (1 + ca) + sa
    x = x + ga * _L0_attn_ref(h, L0_attn_wq, L0_attn_bq, L0_attn_wk, L0_attn_bk, L0_attn_wv, L0_attn_bv, L0_attn_wl, L0_attn_bl)
    h = _layernorm(x, axis=-1) * (1 + cb) + sb
    x = x + gb * _L0_ffn_ref(h, L0_ffn_gate, L0_ffn_kernel, L0_ffn_bias, L0_ffn_lora_A, L0_ffn_lora_B, L0_ffn_lora_A_shared, L0_ffn_lora_B_shared)
    return x

_drawn_inputs = setup_inputs


def setup_inputs(seed=0):
    import zlib

    import numpy as np

    out = dict(_drawn_inputs(seed))
    spreads = {'L0_ffn_bias': (0.0, 1.196)}
    factors = {'L0_attn_wq': 8.0,
     'L0_attn_bq': 8.0,
     'L0_attn_wk': 8.0,
     'L0_attn_bk': 8.0,
     'L0_attn_wv': 2.732,
     'L0_attn_bv': 8.0,
     'L0_ffn_gate': 3.9,
     'L0_ffn_lora_A': 4.144,
     'L0_ffn_lora_B': 4.155,
     'L0_ffn_lora_A_shared': 4.147,
     'L0_ffn_lora_B_shared': 4.156}
    for name, (base, spread) in spreads.items():
        noise = np.random.default_rng([zlib.crc32(name.encode()), seed]).standard_normal(out[name].shape)
        drawn = base * np.exp(spread * noise) if base else spread * noise
        out[name] = jnp.asarray(drawn.astype(out[name].dtype))
    for name, factor in factors.items():
        out[name] = (out[name] * factor).astype(out[name].dtype)
    return out
```

```python
from contextlib import ExitStack

import concourse.bass as bass
from concourse import mybir

F32 = mybir.dt.float32
ALU = mybir.AluOpType
ACT = mybir.ActivationFunctionType
AX_X = mybir.AxisListType.X
AX_XY = mybir.AxisListType.XY

P = 128
BANKS = 8
BANK = 512
EPS = 1e-5
GATE_FLOOR = 0.25


def bank_plan(NB, IC, NHG, NS):
    half = NB // 2
    uses = [("mod_attn", 0, "v")]
    uses += [("wq_t", i, "a") for i in range(IC)]
    uses += [("h_t", i, "a") for i in range(IC)]
    uses += [("q", j, "v") for j in range(half)]
    uses += [("h_t", IC + i, "a") for i in range(IC)]
    uses += [("q", j, "v") for j in range(half, NB)]
    uses += [("wk_t", i, "a") for i in range(IC)]
    uses += [("mod_ffn", 0, "v"), ("gate_attn", 0, "v"), ("gate_ffn", 0, "v")]
    uses += [("q_t", i, "a") for i in range(NHG)]
    uses += [("k", j, "v") for j in range(NB)]
    uses += [("wv_t", i, "a") for i in range(IC)]
    uses += [("k_t", i, "va"[i % 2]) for i in range(NHG)]
    uses += [("v", 0, "v"), ("v", 1, "v")]
    for s in range(NS):
        uses += [("scores", s, "a")]
        if s % 2 and s // 2 + 2 < NB:
            uses += [("v", s // 2 + 2, "v")]
    uses += [("v_t", i, "a") for i in range(NHG)]
    uses += [("ctx", s, "v") for s in range(NS)]
    uses += [("ctx_t", i, "v") for i in range(NHG)]
    uses += [("as_t", 0, "a"), ("bs_t", 0, "a")]
    uses += [("b_t", i, "a") for i in range(IC)]
    uses += [("a_eff", i, "a") for i in range(IC // 2)]
    uses += [("b_eff", i, "a") for i in range(2)]
    uses += [("h2_t", 0, "a")]
    for j in range(NB):
        if j + 1 < NB:
            uses += [("h2_t", j + 1, "a")]
        uses += [("ax", j, "a"), ("out", j, "v")]
    return uses


def adaln_block(nc, x, wq, bq, wk, bk, wv, bv, gate, kern, bias, lora_a, lora_b, lora_as, lora_bs, cond, wmod, out):
    tokens, hid = x.shape[1], x.shape[2]
    lora_n, rank = lora_a.shape[0], lora_a.shape[1]
    D = 16
    H = hid // D
    NB = tokens // P
    IC = hid // P
    HALF = 2
    SLOT = NB // HALF
    NHG = H // 4
    GB = BANK // (HALF * H)
    NS = P // GB
    NCH = NS // 2
    CH = 2 * BANK
    RCH = CH // H
    SCALE = float(D) ** -0.5
    W = IC * hid
    NBH = NB // 2
    assert NB == 8 and IC == 4 and H == 32 and gate.shape[0] == NB and lora_n * rank == hid and rank == 32
    NG = P // rank

    uses = bank_plan(NB, IC, NHG, NS)
    use_no = {(s, i): u for u, (s, i, _) in enumerate(uses)}

    with ExitStack() as ctx:
        def sb(name, cols):
            return ctx.enter_context(nc.sbuf_tensor(name, [P, cols], F32))

        def sem(name):
            return ctx.enter_context(nc.semaphore(name))

        diag = sb("diag", SLOT * H * P)
        kp = sb("kp", HALF * H * P)
        sreg = sb("sreg", HALF * H * P)
        nat = sb("nat", NB * hid)
        xres = sb("xres", NB * hid)
        hT = sb("hT", NB * hid)
        wA = sb("wA", W)
        wB = sb("wB", W)
        bq_bc = sb("bq_bc", hid)
        bk_bc = sb("bk_bc", hid)
        bv_bc = sb("bv_bc", hid)
        ga_bc = sb("ga_bc", hid)
        gb_bc = sb("gb_bc", hid)
        ident = sb("ident", P)
        half_mask = sb("half_mask", HALF)
        d_mask = sb("d_mask", D)
        ga_col = sb("ga_col", H)
        rank_mask = sb("rank_mask", rank)
        gate_col = sb("gate_col", IC * NB)
        silu = sb("silu", 4 * IC)
        cbc = sb("cbc", IC * P)
        modc = sb("modc", 4 * IC)
        axT = sb("axT", 2 * P)
        stats = sb("stats", NB * 6)
        mv = sb("mv", NB * 2)
        std = sb("std", NB)
        rstd = sb("rstd", NB)
        rmax = sb("rmax", 2 * RCH)
        rsum = sb("rsum", 2 * RCH)
        rinv = sb("rinv", 2 * RCH)
        ps = ctx.enter_context(nc.psum_tensor("ps", [P, BANKS * BANK], F32))

        x_v = xres[:].rearrange("p (j n) -> p j n", j=NB)
        x_hjd = xres[:].rearrange("p (j h d) -> p h j d", j=NB, d=D)
        xn_v = diag[:, (SLOT - 1) * H * P:].rearrange("p (j n) -> p j n", j=NB)
        hT_v = hT[:].rearrange("p (c t) -> p c t", c=IC)
        wm_attn = kp[:, 0:2 * W].rearrange("p (c n) -> p c n", c=IC)
        wm_rest = sreg[:].rearrange("p (c n) -> p c n", c=IC)
        wq_nat = kp[:, 2 * W:3 * W].rearrange("p (c n) -> p c n", c=IC)
        wk_nat = kp[:, 3 * W:4 * W].rearrange("p (c n) -> p c n", c=IC)
        wv_nat = wq_nat
        wA_v = wA[:].rearrange("p (c n) -> p c n", c=IC)
        wB_v = wB[:].rearrange("p (c n) -> p c n", c=IC)
        q_nat = nat[:].rearrange("p (h j d) -> p h j d", j=NB, d=D)
        k_nat_r = sreg[:, NB * hid:2 * NB * hid]
        k_nat = k_nat_r.rearrange("p (h j d) -> p h j d", j=NB, d=D)
        v_nat = nat[:].rearrange("p (f d s t) -> p f s t d", f=HALF, d=D, s=SLOT)
        qc = sreg[:, 0:NB * hid]
        k2 = kp[:].rearrange("p (f h g) -> p f h g", f=HALF, g=P)
        diag_s = diag[:].rearrange("p (s n) -> p s n", s=SLOT)
        diag_g = diag[:].rearrange("p (m g) -> p m g", g=P)
        k2_g = kp[:].rearrange("p (n g) -> p n g", g=P)
        pT_g = kp[:].rearrange("p (g n) -> p g n", g=P)
        s_rows = sreg[:].rearrange("p (c r t) -> p c r t", c=NCH, t=H)
        ctx_c = nat[:].rearrange("p (h g) -> p h g", g=P)
        ctx_w = nat[:].rearrange("p (h g) -> p g h", g=P)
        xn2 = nat[:].rearrange("p (j n) -> p j n", j=NB)
        h2T = kp[:, 0:NB * hid].rearrange("p (j c t) -> p j c t", j=NB, c=IC)
        la_nat = wB_v
        as_nat = bq_bc
        bs_nat = bk_bc[:, 0:IC * rank].rearrange("p (c r) -> p c r", c=IC)
        b_tail = ga_bc
        b_t = hT[:, 0:W].rearrange("p (c o) -> p c o", c=IC)
        a_cat = hT[:, W:2 * W].rearrange("p (c b r) -> p c b r", c=IC, b=NB)
        b_cat = sreg[:, 0:NB * hid].rearrange("p (b o) -> p b o", b=NB)
        o = NB * hid
        b_raw = sreg[:, o:o + 2 * hid].rearrange("p (q o) -> p q o", q=2)
        o += 2 * hid
        sign_tmp = kp[:, 0:hid]
        gmix = sreg[:, o:o + IC * NB * rank].rearrange("p (c n) -> p c n", c=IC)
        o += IC * NB * rank
        lb_nat = sreg[:, o:o + W].rearrange("p (c n) -> p c n", c=IC)

        psum_written = sem("psum_written")
        dve_emptied = sem("dve_emptied")
        act_emptied = sem("act_emptied")
        dve_chain = sem("dve_chain")
        pool_chain = sem("pool_chain")
        cond_in = sem("cond_in")
        wm_attn_in = sem("wm_attn_in")
        wm_rest_in = sem("wm_rest_in")
        x_in = [sem(f"x_in{j}") for j in range(NB)]
        wq_in = sem("wq_in")
        wk_in = sem("wk_in")
        wv_in = sem("wv_in")
        bqk_in = sem("bqk_in")
        bv_in = sem("bv_in")
        gate_in = sem("gate_in")
        kern_in = sem("kern_in")
        la_in = sem("la_in")
        lb_in = sem("lb_in")
        lsh_in = sem("lsh_in")
        bias_in = sem("bias_in")
        q_diag_in = sem("q_diag_in")
        v_diag_in = sem("v_diag_in")
        b_tail_in = sem("b_tail_in")
        b_eff_in = sem("b_eff_in")
        out_sent = sem("out_sent")
        ident_made = sem("ident_made")
        diag_zero = sem("diag_zero")
        exp_c = sem("exp_c")
        silu_made = sem("silu_made")
        var_ready = sem("var_ready")
        std_ready = sem("std_ready")
        xn_ready = sem("xn_ready")
        shifted = sem("shifted")
        exped = sem("exped")
        inv_ready = sem("inv_ready")
        normed = sem("normed")
        turned = sem("turned")
        ga_ready = sem("ga_ready")
        ctx_gated = sem("ctx_gated")
        ctx_low = sem("ctx_low")
        gmix_made = sem("gmix_made")
        kern_scaled = sem("kern_scaled")
        b_scaled = sem("b_scaled")
        tail_scaled = sem("tail_scaled")
        ones_made = sem("ones_made")

        def bank(stage, i):
            b = use_no[stage, i] % BANKS
            return ps[:, b * BANK:(b + 1) * BANK]

        def written(stage, i):
            return use_no[stage, i] + 1

        def emptied(stage, i):
            u = use_no[stage, i]
            who = uses[u][2]
            return (dve_emptied if who == "v" else act_emptied), sum(1 for w in uses[:u + 1] if w[2] == who)

        block = ctx.enter_context(nc.Block())

        @block.sync
        def _(sp):
            sp.dma_start(silu[:, 0:IC], cond[0].rearrange("(c p) -> p c", p=P), allow_slow_non_contiguous=True).then_inc(cond_in, 16)
            wm = wmod.rearrange("(c p) n -> p c n", p=P)
            xr = x[0].rearrange("(j p) n -> p j n", p=P)
            sp.dma_start(wm_attn, wm[:, :, 0:2 * hid]).then_inc(wm_attn_in, 16)
            for j in range(NBH):
                sp.dma_start(x_v[:, j, :], xr[:, j, :]).then_inc(x_in[j], 16)
            sp.dma_start(wq_nat, wq.rearrange("(c p) n -> p c n", p=P)).then_inc(wq_in, 16)
            for j in range(NBH, NB):
                sp.dma_start(x_v[:, j, :], xr[:, j, :]).then_inc(x_in[j], 16)
            sp.dma_start(wk_nat, wk.rearrange("(c p) n -> p c n", p=P)).then_inc(wk_in, 16)
            sp.dma_start(wm_rest, wm[:, :, 2 * hid:6 * hid]).then_inc(wm_rest_in, 16)
            sp.wait_ge(psum_written, written("wq_t", IC - 1))
            sp.dma_start(wv_nat, wv.rearrange("(c p) n -> p c n", p=P)).then_inc(wv_in, 16)
            sp.wait_ge(*emptied("q_t", NHG - 1))
            sp.wait_ge(diag_zero, 2)
            for s in range(SLOT):
                r = slice(32 * s, 32 * s + 32)
                sp.dma_start(diag_s[r, s, :], qc[r, :]).then_inc(q_diag_in, 16)
            sp.wait_ge(*emptied("q", NB - 1))
            sp.dma_start(as_nat[0:rank, :], lora_as[:, :]).then_inc(lsh_in, 16)
            sp.wait_ge(*emptied("k", NB - 1))
            sp.dma_start(bs_nat, lora_bs.rearrange("(c p) r -> p c r", p=P)).then_inc(lsh_in, 16)
            sp.wait_ge(psum_written, written("k", NB - 1))
            sp.dma_start(la_nat, lora_a.rearrange("(c n) r i -> (n r) c i", n=NG)).then_inc(la_in, 16)
            sp.wait_ge(ga_ready, 1)
            sp.dma_start(b_tail[2 * rank:2 * rank + 1, :], bias.rearrange("(a n) -> a n", a=1)).then_inc(bias_in, 16)
            sp.wait_ge(psum_written, written("v", NB - 1))
            sp.dma_start(wA_v, kern.rearrange("(c p) n -> p c n", p=P)).then_inc(kern_in, 16)
            sp.wait_ge(psum_written, written("scores", NS - 1))
            sp.wait_ge(*emptied("v_t", NHG - 1))
            for s in range(SLOT):
                r = slice(32 * s, 32 * s + 32)
                sp.dma_start(diag_s[r, s, :], hT[r, :]).then_inc(v_diag_in, 16)
            sp.wait_ge(turned, NCH)
            for c in range(IC):
                sp.dma_start(lb_nat[:, c, :].rearrange("p (n r) -> p n r", r=rank),
                             lora_b[:, c * P:(c + 1) * P, :].rearrange("n p r -> p n r")).then_inc(lb_in, 16)
            sp.wait_ge(tail_scaled, 2)
            rows = slice(rank, 2 * rank)
            sp.dma_start(b_cat[rows], b_tail[rows, :].unsqueeze(1).to_broadcast([rank, NB, hid])).then_inc(b_tail_in, 16)
            rows = slice(2 * rank, 2 * rank + 1)
            sp.dma_start(b_cat[rows], b_tail[rows, :].unsqueeze(1).to_broadcast([1, NB, hid])).then_inc(b_tail_in, 16)
            sp.wait_ge(b_scaled, 1)
            for b in range(NB):
                r = slice(32 * (b % 4), 32 * (b % 4) + 32)
                sp.dma_start(b_cat[0:rank, b, :], b_raw[r, b // 4, :]).then_inc(b_eff_in, 16)
            orow = out[0].rearrange("(j p) n -> p j n", p=P)
            for j in range(NB):
                sp.wait_ge(*emptied("out", j))
                sp.dma_start(orow[:, j, :], x_v[:, j, :]).then_inc(out_sent, 16)
            sp.wait_ge(out_sent, 16 * NB)

        @block.gpsimd
        def _(pool):
            nc.gpsimd.memset(ident[:], 0.0).then_inc(pool_chain, 1)
            pool.wait_ge(pool_chain, 1)
            nc.gpsimd.affine_select(out=ident[:], in_=ident[:], compare_op=ALU.not_equal, fill=1.0, base=0,
                                    pattern=[[-1, P]], channel_multiplier=1).then_inc(ident_made, 1)
            nc.gpsimd.memset(diag[:, 0:(SLOT - 1) * H * P], 0.0).then_inc(diag_zero, 1)
            pool.wait_ge(psum_written, written("h_t", 2 * IC - 1))
            nc.gpsimd.memset(diag[:, (SLOT - 1) * H * P:], 0.0).then_inc(diag_zero, 1)
            for c in range(NCH):
                b = c % 2
                pool.wait_ge(inv_ready, c + 1)
                nc.gpsimd.tensor_tensor(s_rows[:, c], s_rows[:, c],
                                        rinv[:, b * RCH:(b + 1) * RCH].unsqueeze(2).to_broadcast([P, RCH, H]),
                                        ALU.mult).then_inc(normed, 1)
            pool.wait_ge(ga_ready, 1)
            for s in range(0, NS, 2):
                pool.wait_ge(*emptied("ctx", s + 1))
                part = ctx_c[:, :, s * GB:(s + 2) * GB]
                nc.gpsimd.tensor_tensor(part, part, ga_col[:].unsqueeze(2).to_broadcast([P, H, 2 * GB]),
                                        ALU.mult).then_inc(ctx_gated, 1)
            pool.wait_ge(turned, NCH)
            pool.wait_ge(gate_in, 16 * NG * IC)
            nc.gpsimd.tensor_tensor(gmix[:].rearrange("p c (b r) -> p (c b) r", r=rank),
                                    gate_col[:].unsqueeze(2).to_broadcast([P, IC * NB, rank]),
                                    rank_mask[:].unsqueeze(1).to_broadcast([P, IC * NB, rank]),
                                    ALU.mult).then_inc(gmix_made, 1)
            pool.wait_ge(kern_in, 16)
            nc.gpsimd.tensor_tensor(wA_v, wA_v, gb_bc[:].unsqueeze(1).to_broadcast([P, IC, hid]),
                                    ALU.mult).then_inc(kern_scaled, 1)
            pool.wait_ge(bias_in, 16)
            pool.wait_ge(kern_scaled, 1)
            r = slice(2 * rank, 2 * rank + 1)
            nc.gpsimd.tensor_tensor(b_tail[r, :], b_tail[r, :], gb_bc[r, :], ALU.mult).then_inc(tail_scaled, 1)
            pool.wait_ge(*emptied("bs_t", 0))
            pool.wait_ge(tail_scaled, 1)
            r = slice(rank, 2 * rank)
            nc.gpsimd.tensor_tensor(b_tail[r, :], b_tail[r, :], gb_bc[r, :], ALU.mult).then_inc(tail_scaled, 1)
            pool.wait_ge(*emptied("b_eff", 1))
            pool.wait_ge(tail_scaled, 2)
            nc.gpsimd.tensor_tensor(b_raw, b_raw, gb_bc[:].unsqueeze(1).to_broadcast([P, 2, hid]),
                                    ALU.mult).then_inc(b_scaled, 1)

        @block.scalar
        def _(act):
            act.dma_start(bq_bc[:], bq.partition_broadcast(P)).then_inc(bqk_in, 16)
            act.dma_start(bk_bc[:], bk.partition_broadcast(P)).then_inc(bqk_in, 16)
            act.dma_start(bv_bc[:], bv.partition_broadcast(P)).then_inc(bv_in, 16)
            for n in range(NG):
                for c in range(IC):
                    act.dma_start(gate_col[rank * n:rank * (n + 1), c * NB:(c + 1) * NB],
                                  gate[:, NG * c + n].partition_broadcast(rank),
                                  allow_slow_non_contiguous=True).then_inc(gate_in, 16)

            def empty(stage, i, dst, src=None):
                act.wait_ge(psum_written, written(stage, i))
                nc.scalar.activation(dst, bank(stage, i) if src is None else src, ACT.Copy).then_inc(act_emptied, 1)

            act.wait_ge(cond_in, 16)
            nc.scalar.activation(silu[:, IC:2 * IC], silu[:, 0:IC], ACT.Exp, scale=-1.0).then_inc(exp_c, 1)
            for i in range(IC):
                empty("wq_t", i, wA_v[:, i, :])

            def h_t(k):
                act.wait_ge(var_ready, k + 1)
                nc.scalar.activation(std[:, k * NBH:(k + 1) * NBH],
                                     mv[:].rearrange("p (j s) -> p j s", s=2)[:, k * NBH:(k + 1) * NBH, 1],
                                     ACT.Sqrt).then_inc(std_ready, 1)
                if k == 0:
                    act.wait_ge(*emptied("mod_attn", 0))
                for i in range(IC):
                    act.wait_ge(psum_written, written("h_t", k * IC + i))
                    nc.scalar.activation(hT_v[:, i, k * NBH * P:(k + 1) * NBH * P], bank("h_t", k * IC + i),
                                         ACT.Identity, bias=modc[:, i:i + 1],
                                         scale=modc[:, IC + i:IC + i + 1]).then_inc(act_emptied, 1)

            h_t(0)
            h_t(1)
            for i in range(IC):
                empty("wk_t", i, wB_v[:, i, :])
            for i in range(NHG):
                empty("q_t", i, qc[:, i * BANK:(i + 1) * BANK])
            for i in range(IC):
                empty("wv_t", i, wA_v[:, i, :])
            for i in range(1, NHG, 2):
                act.wait_ge(psum_written, written("k_t", i))
                for f in range(HALF):
                    ins = nc.scalar.activation(k2[:, f, 4 * i:4 * i + 4, :],
                                               bank("k_t", i).rearrange("p (h g) -> p h g", g=P),
                                               ACT.Copy, scale=half_mask[:, f:f + 1])
                ins.then_inc(act_emptied, 1)

            def exp_chunk(c):
                act.wait_ge(shifted, c + 1)
                nc.scalar.activation(s_rows[:, c], s_rows[:, c], ACT.Exp, scale=SCALE).then_inc(exped, 1)

            act.wait_ge(q_diag_in, 16 * SLOT)
            for c in range(NCH):
                for s in (2 * c, 2 * c + 1):
                    empty("scores", s, sreg[:, s * BANK:(s + 1) * BANK])
                if c:
                    exp_chunk(c - 1)
            exp_chunk(NCH - 1)
            for i in range(NHG):
                empty("v_t", i, hT[:, i * BANK:(i + 1) * BANK])
            act.wait_ge(psum_written, written("v_t", NHG - 1))
            for s in range(NS):
                act.wait_ge(psum_written, written("ctx", s))
                nc.scalar.activation(ctx_w[:, s * GB:(s + 1) * GB, :],
                                     bank("ctx", s).rearrange("p (g f h) -> p g f h", f=HALF, h=H)[:, :, 0, :],
                                     ACT.Copy, scale=half_mask[:, 0:1]).then_inc(ctx_low, 1)
            act.wait_ge(v_diag_in, 16 * SLOT)
            act.wait_ge(psum_written, written("as_t", 0))
            nc.scalar.activation(a_cat[:, :, :, rank:2 * rank],
                                 bank("as_t", 0)[:, 0:IC * rank].rearrange("p (c r) -> p c r", c=IC)
                                 .unsqueeze(2).to_broadcast([P, IC, NB, rank]), ACT.Copy).then_inc(act_emptied, 1)
            act.wait_ge(ga_ready, 1)
            empty("bs_t", 0, b_tail[rank:2 * rank, :], bank("bs_t", 0)[0:rank, :])
            for i in range(IC):
                empty("b_t", i, b_t[:, i, :])
            for i in range(IC // 2):
                empty("a_eff", i, a_cat[:, 2 * i:2 * i + 2, :, 0:rank],
                      bank("a_eff", i).rearrange("p (c b r) -> p c b r", c=2, b=NB))
            for i in range(2):
                empty("b_eff", i, b_raw[:, i, :])

            def h2_t(j):
                act.wait_ge(psum_written, written("h2_t", j))
                for c in range(IC):
                    ins = nc.scalar.activation(h2T[:, j, c, :], bank("h2_t", j)[:, c * P:(c + 1) * P], ACT.Identity,
                                               bias=modc[:, 2 * IC + c:2 * IC + c + 1],
                                               scale=modc[:, 3 * IC + c:3 * IC + c + 1])
                ins.then_inc(act_emptied, 1)

            for k in range(2):
                act.wait_ge(var_ready, 3 + k)
                nc.scalar.activation(std[:, k * NBH:(k + 1) * NBH],
                                     mv[:].rearrange("p (j s) -> p j s", s=2)[:, k * NBH:(k + 1) * NBH, 1],
                                     ACT.Sqrt).then_inc(std_ready, 1)
            act.wait_ge(*emptied("mod_ffn", 0))
            h2_t(0)
            for j in range(NB):
                if j + 1 < NB:
                    h2_t(j + 1)
                if j >= 2:
                    act.wait_ge(psum_written, written("out", j - 2))
                empty("ax", j, axT[0:2 * rank, (j % 2) * P:(j % 2 + 1) * P], bank("ax", j)[0:2 * rank, 0:P])

        @block.vector
        def _(dve):
            chain = [0]

            def link(ins):
                chain[0] += 1
                ins.then_inc(dve_chain, 1)
                dve.wait_ge(dve_chain, chain[0])

            mv_v = mv[:].rearrange("p (j s) -> p j s", s=2)

            nc.vector.memset(axT[2 * rank:2 * rank + 1, :], 1.0).then_inc(ones_made, 1)
            dve.wait_ge(exp_c, 1)
            link(nc.vector.tensor_scalar(silu[:, 2 * IC:3 * IC], silu[:, IC:2 * IC], 1.0, None, ALU.add))
            link(nc.vector.reciprocal(silu[:, 3 * IC:4 * IC], silu[:, 2 * IC:3 * IC]))
            link(nc.vector.tensor_tensor(silu[:, 2 * IC:3 * IC], silu[:, 0:IC], silu[:, 3 * IC:4 * IC], ALU.mult))
            nc.vector.tensor_copy(cbc[:].rearrange("p (c m) -> p c m", c=IC),
                                  silu[:, 2 * IC:3 * IC].unsqueeze(2).to_broadcast([P, IC, P])).then_inc(silu_made, 1)
            dve.wait_ge(ident_made, 1)
            nc.vector.tensor_reduce(half_mask[:], ident[:].rearrange("p (s f d) -> p f s d", f=HALF, d=D), AX_XY, ALU.add)
            nc.vector.tensor_reduce(d_mask[:], ident[:].rearrange("p (j d) -> p d j", d=D), AX_X, ALU.add)
            link(nc.vector.tensor_reduce(rank_mask[:], ident[:].rearrange("p (n r) -> p r n", r=rank), AX_X, ALU.add))

            def layer_norm_stats(j0, j1):
                for j in range(j0, j1):
                    ins = nc.vector.bn_stats(stats[:, 6 * j:6 * j + 6], x_v[:, j, :])
                link(ins)
                for j in range(j0, j1):
                    ins = nc.vector.bn_aggr(mv_v[:, j, :], stats[:, 6 * j:6 * j + 6])
                link(ins)
                nc.vector.tensor_scalar(mv_v[:, j0:j1, 1], mv_v[:, j0:j1, 1], EPS, None, ALU.add).then_inc(var_ready, 1)

            def normalise(k, dst):
                j0, j1 = (k % 2) * NBH, (k % 2 + 1) * NBH
                dve.wait_ge(std_ready, k + 1)
                link(nc.vector.reciprocal(rstd[:, j0:j1], std[:, j0:j1]))
                for j in range(j0, j1):
                    nc.vector.tensor_scalar(dst[:, j, :], x_v[:, j, :], mv_v[:, j, 0:1], rstd[:, j:j + 1],
                                            ALU.subtract, ALU.mult).then_inc(xn_ready, 1)

            for j in range(NBH):
                dve.wait_ge(x_in[j], 16)
            layer_norm_stats(0, NBH)
            dve.wait_ge(psum_written, written("mod_attn", 0))
            nc.vector.tensor_copy(modc[:, 0:IC], bank("mod_attn", 0)[:, 0:IC])
            nc.vector.tensor_scalar(modc[:, IC:2 * IC], bank("mod_attn", 0)[:, IC:2 * IC], 1.0, None,
                                    ALU.add).then_inc(dve_emptied, 1)
            normalise(0, xn_v)
            for j in range(NBH, NB):
                dve.wait_ge(x_in[j], 16)
            layer_norm_stats(NBH, NB)
            normalise(1, xn_v)
            dve.wait_ge(bqk_in, 32)
            for j in range(NB):
                dve.wait_ge(psum_written, written("q", j))
                nc.vector.tensor_tensor(q_nat[:, :, j, :], bank("q", j).rearrange("p (h d) -> p h d", d=D),
                                        bq_bc[:].rearrange("p (h d) -> p h d", d=D), ALU.add).then_inc(dve_emptied, 1)
            dve.wait_ge(psum_written, written("mod_ffn", 0))
            nc.vector.tensor_copy(modc[:, 2 * IC:3 * IC], bank("mod_ffn", 0)[:, 0:IC])
            nc.vector.tensor_scalar(modc[:, 3 * IC:4 * IC], bank("mod_ffn", 0)[:, IC:2 * IC], 1.0, None,
                                    ALU.add).then_inc(dve_emptied, 1)
            for name, dst in (("gate_attn", ga_bc), ("gate_ffn", gb_bc)):
                dve.wait_ge(psum_written, written(name, 0))
                link(nc.vector.tensor_scalar(sign_tmp, bank(name, 0), 0.0, 2.0, ALU.is_ge, ALU.mult))
                nc.vector.scalar_tensor_tensor(out=dst[:], in0=sign_tmp, scalar=-1.0, in1=bank(name, 0),
                                               op0=ALU.add, op1=ALU.mult).then_inc(dve_emptied, 1)
                dve.wait_ge(*emptied(name, 0))
                link(nc.vector.tensor_scalar(dst[:], dst[:], GATE_FLOOR, None, ALU.max))
                link(nc.vector.scalar_tensor_tensor(out=dst[:], in0=sign_tmp, scalar=-1.0, in1=dst[:],
                                                    op0=ALU.add, op1=ALU.mult))
            link(nc.vector.tensor_tensor(sign_tmp.rearrange("p (h d) -> p h d", d=D),
                                         ga_bc[:].rearrange("p (h d) -> p h d", d=D),
                                         d_mask[:].unsqueeze(1).to_broadcast([P, H, D]), ALU.mult))
            nc.vector.tensor_reduce(ga_col[:], sign_tmp.rearrange("p (h d) -> p h d", d=D), AX_X,
                                    ALU.add).then_inc(ga_ready, 1)
            for j in range(NB):
                dve.wait_ge(psum_written, written("k", j))
                nc.vector.tensor_tensor(k_nat[:, :, j, :], bank("k", j).rearrange("p (h d) -> p h d", d=D),
                                        bk_bc[:].rearrange("p (h d) -> p h d", d=D), ALU.add).then_inc(dve_emptied, 1)
            for i in range(0, NHG, 2):
                dve.wait_ge(psum_written, written("k_t", i))
                for f in range(HALF):
                    ins = nc.vector.tensor_scalar(k2[:, f, 4 * i:4 * i + 4, :],
                                                  bank("k_t", i).rearrange("p (h g) -> p h g", g=P),
                                                  half_mask[:, f:f + 1], None, ALU.mult)
                ins.then_inc(dve_emptied, 1)

            def take_v(j):
                dve.wait_ge(psum_written, written("v", j))
                nc.vector.tensor_tensor(v_nat[:, j % HALF, j // HALF], bank("v", j).rearrange("p (h d) -> p h d", d=D),
                                        bv_bc[:].rearrange("p (h d) -> p h d", d=D), ALU.add).then_inc(dve_emptied, 1)

            def row_max(c):
                b = c % 2
                dve.wait_ge(*emptied("scores", 2 * c + 1))
                m = rmax[:, b * RCH:(b + 1) * RCH]
                link(nc.vector.tensor_reduce(m, s_rows[:, c], AX_X, ALU.max))
                nc.vector.tensor_tensor(s_rows[:, c], s_rows[:, c], m.unsqueeze(2).to_broadcast([P, RCH, H]),
                                        ALU.subtract).then_inc(shifted, 1)

            def row_sum(c):
                b = c % 2
                dve.wait_ge(exped, c + 1)
                link(nc.vector.tensor_reduce(rsum[:, b * RCH:(b + 1) * RCH], s_rows[:, c], AX_X, ALU.add))
                if c >= 2:
                    dve.wait_ge(normed, c - 1)
                nc.vector.reciprocal(rinv[:, b * RCH:(b + 1) * RCH], rsum[:, b * RCH:(b + 1) * RCH]).then_inc(inv_ready, 1)

            dve.wait_ge(bv_in, 16)
            take_v(0)
            take_v(1)
            for c in range(NCH):
                if c + 2 < NB:
                    take_v(c + 2)
                row_max(c)
                if c:
                    row_sum(c - 1)
            row_sum(NCH - 1)

            dve.wait_ge(psum_written, written("scores", NS - 1))
            for c in range(NCH):
                dve.wait_ge(normed, c + 1)
                nc.vector.transpose(kp[:, c * CH:(c + 1) * CH], sreg[:, c * CH:(c + 1) * CH]).then_inc(turned, 1)
            for s in range(NS):
                dve.wait_ge(ctx_low, s + 1)
                dst = ctx_w[:, s * GB:(s + 1) * GB, :]
                nc.vector.scalar_tensor_tensor(
                    out=dst, in0=bank("ctx", s).rearrange("p (g f h) -> p g f h", f=HALF, h=H)[:, :, 1, :],
                    scalar=half_mask[:, 1:2], in1=dst, op0=ALU.mult, op1=ALU.add).then_inc(dve_emptied, 1)
            for i in range(NHG):
                dve.wait_ge(psum_written, written("ctx_t", i))
                dst = x_hjd[:, 4 * i:4 * i + 4]
                nc.vector.tensor_tensor(dst, bank("ctx_t", i).rearrange("p (h j d) -> p h j d", h=4, d=D), dst,
                                        ALU.add).then_inc(dve_emptied, 1)
            dve.wait_ge(*emptied("ctx_t", NHG - 1))
            layer_norm_stats(0, NBH)
            layer_norm_stats(NBH, NB)
            normalise(2, xn2)
            normalise(3, xn2)
            for j in range(NB):
                dve.wait_ge(psum_written, written("out", j))
                nc.vector.tensor_tensor(x_v[:, j, :], bank("out", j), x_v[:, j, :], ALU.add).then_inc(dve_emptied, 1)

        @block.tensor
        def _(pe):
            def take(stage, i):
                u = use_no[stage, i]
                if u >= BANKS:
                    pe.wait_ge(*emptied(*uses[u - BANKS][0:2]))
                return bank(stage, i)

            def mod_columns(stage, w, cols):
                dst = take(stage, 0)
                for n, o0 in enumerate(cols):
                    for c in range(IC):
                        ins = nc.tensor.matmul(dst[:, n:n + 1], w[:, c, o0:o0 + P], silu[:, 2 * IC + c:2 * IC + c + 1],
                                               start=(c == 0), stop=(c == IC - 1))
                ins.then_inc(psum_written, 1)

            def gate_rows(stage, o0):
                dst = take(stage, 0)
                for c in range(IC):
                    ins = nc.tensor.matmul(dst, cbc[:, c * P:(c + 1) * P], wm_rest[:, c, o0:o0 + hid],
                                           start=(c == 0), stop=(c == IC - 1))
                ins.then_inc(psum_written, 1)

            def transposes(stage, i, blocks):
                dst = take(stage, i)
                for n, src in enumerate(blocks):
                    k, m = src.shape[0], src.shape[1]
                    ins = nc.tensor.transpose(dst[0:m, n * k:(n + 1) * k], src, ident[0:k, 0:k])
                ins.then_inc(psum_written, 1)

            def weight_t(stage, w_nat):
                for i in range(IC):
                    transposes(stage, i, [w_nat[:, c, i * P:(i + 1) * P] for c in range(IC)])

            def project(stage, j, w):
                dst = take(stage, j)
                for c in range(IC):
                    ins = nc.tensor.matmul(dst, hT_v[:, c, j * P:(j + 1) * P], w[:, c, :],
                                           start=(c == 0), stop=(c == IC - 1))
                ins.then_inc(psum_written, 1)

            pe.wait_ge(silu_made, 1)
            pe.wait_ge(wm_attn_in, 16)
            mod_columns("mod_attn", wm_attn, [s * hid + c * P for s in range(2) for c in range(IC)])
            pe.wait_ge(ident_made, 1)
            pe.wait_ge(wq_in, 16)
            weight_t("wq_t", wq_nat)
            for k in range(2):
                pe.wait_ge(xn_ready, (k + 1) * NBH)
                for i in range(IC):
                    transposes("h_t", k * IC + i,
                               [xn_v[:, j, i * P:(i + 1) * P] for j in range(k * NBH, (k + 1) * NBH)])
                pe.wait_ge(*emptied("h_t", k * IC + IC - 1))
                for j in range(k * NBH, (k + 1) * NBH):
                    project("q", j, wA_v)
            pe.wait_ge(wk_in, 16)
            weight_t("wk_t", wk_nat)
            pe.wait_ge(wm_rest_in, 16)
            mod_columns("mod_ffn", wm_rest, [(1 + s) * hid + c * P for s in range(2) for c in range(IC)])
            gate_rows("gate_attn", 0)
            gate_rows("gate_ffn", 3 * hid)
            pe.wait_ge(*emptied("q", NB - 1))
            for i in range(NHG):
                transposes("q_t", i, [nat[:, h * P:(h + 1) * P] for h in range(4 * i, 4 * i + 4)])
            pe.wait_ge(*emptied("wk_t", IC - 1))
            for j in range(NB):
                project("k", j, wB_v)
            pe.wait_ge(wv_in, 16)
            weight_t("wv_t", wv_nat)
            pe.wait_ge(*emptied("k", NB - 1))
            for i in range(NHG):
                transposes("k_t", i, [k_nat_r[:, h * P:(h + 1) * P] for h in range(4 * i, 4 * i + 4)])
            pe.wait_ge(*emptied("wv_t", IC - 1))
            project("v", 0, wA_v)
            project("v", 1, wA_v)
            pe.wait_ge(q_diag_in, 16 * SLOT)
            pe.wait_ge(*emptied("k_t", NHG - 2))
            pe.wait_ge(*emptied("k_t", NHG - 1))
            for s in range(NS):
                dst = take("scores", s)
                for n in range(GB):
                    g = s * GB + n
                    ins = nc.tensor.matmul(dst[:, n * HALF * H:(n + 1) * HALF * H], diag_g[:, :, g], k2_g[:, :, g],
                                           start=True, stop=True)
                ins.then_inc(psum_written, 1)
                if s % 2 and s // 2 + 2 < NB:
                    project("v", s // 2 + 2, wA_v)
            pe.wait_ge(*emptied("v", NB - 1))
            for i in range(NHG):
                transposes("v_t", i, [nat[:, n * P:(n + 1) * P] for n in range(4 * i, 4 * i + 4)])
            pe.wait_ge(v_diag_in, 16 * SLOT)
            for s in range(NS):
                if s % 2 == 0:
                    pe.wait_ge(turned, s // 2 + 1)
                dst = take("ctx", s)
                for n in range(GB):
                    g = s * GB + n
                    ins = nc.tensor.matmul(dst[:, n * HALF * H:(n + 1) * HALF * H], diag_g[:, :, g], pT_g[:, g, :],
                                           start=True, stop=True)
                ins.then_inc(psum_written, 1)
            pe.wait_ge(ctx_gated, NS // 2)
            for i in range(NHG):
                transposes("ctx_t", i, [ctx_c[:, h, :] for h in range(4 * i, 4 * i + 4)])

            pe.wait_ge(lsh_in, 32)
            transposes("as_t", 0, [as_nat[0:rank, c * P:(c + 1) * P] for c in range(IC)])
            transposes("bs_t", 0, [bs_nat[:, c, :] for c in range(IC)])
            pe.wait_ge(lb_in, 16 * IC)
            weight_t("b_t", lb_nat)
            pe.wait_ge(la_in, 16)
            pe.wait_ge(gmix_made, 1)
            for i in range(IC // 2):
                dst = take("a_eff", i)
                for n in range(2):
                    ic = 2 * i + n
                    for c in range(IC):
                        ins = nc.tensor.matmul(dst[:, n * NB * rank:(n + 1) * NB * rank],
                                               la_nat[:, c, ic * P:(ic + 1) * P], gmix[:, c, :],
                                               start=(c == 0), stop=(c == IC - 1))
                ins.then_inc(psum_written, 1)
            pe.wait_ge(*emptied("b_t", IC - 1))
            for i in range(2):
                dst = take("b_eff", i)
                for c in range(IC):
                    ins = nc.tensor.matmul(dst, gmix[:, c, i * P:(i + 1) * P], b_t[:, c, :],
                                           start=(c == 0), stop=(c == IC - 1))
                ins.then_inc(psum_written, 1)

            def h2_t(j):
                pe.wait_ge(xn_ready, NB + j + 1)
                transposes("h2_t", j, [xn2[:, j, c * P:(c + 1) * P] for c in range(IC)])

            h2_t(0)
            for j in range(NB):
                if j + 1 < NB:
                    h2_t(j + 1)
                pe.wait_ge(*emptied("h2_t", j))
                if j == 0:
                    pe.wait_ge(*emptied("a_eff", IC // 2 - 1))
                dst = take("ax", j)[0:2 * rank, 0:P]
                for c in range(IC):
                    ins = nc.tensor.matmul(dst, a_cat[:, c, j, :], h2T[:, j, c, :], start=(c == 0), stop=(c == IC - 1))
                ins.then_inc(psum_written, 1)
                if j == 0:
                    pe.wait_ge(kern_scaled, 1)
                dst = take("out", j)
                for c in range(IC):
                    nc.tensor.matmul(dst, h2T[:, j, c, :], wA_v[:, c, :], start=(c == 0), stop=False)
                if j == 0:
                    pe.wait_ge(ones_made, 1)
                    pe.wait_ge(b_tail_in, 32)
                    pe.wait_ge(b_eff_in, 16 * NB)
                pe.wait_ge(*emptied("ax", j))
                rows = 2 * rank + 1
                nc.tensor.matmul(dst, axT[0:rows, (j % 2) * P:(j % 2 + 1) * P], b_cat[0:rows, j, :],
                                 start=False, stop=True).then_inc(psum_written, 1)


_INS = ["L0_attn_hidden_states", "L0_attn_wq", "L0_attn_bq", "L0_attn_wk", "L0_attn_bk", "L0_attn_wv", "L0_attn_bv",
        "L0_ffn_gate", "L0_ffn_kernel", "L0_ffn_bias", "L0_ffn_lora_A", "L0_ffn_lora_B", "L0_ffn_lora_A_shared",
        "L0_ffn_lora_B_shared", "L0_c", "L0_wmod"]
_OUTS = [((1, 1024, 512), "float32")]


def kernel(**inputs):
    import numpy as _np
    import concourse.bacc as _bacc
    from concourse import mybir as _mybir
    from concourse.bass_utils import run_bass_kernel_spmd as _run

    nc = _bacc.Bacc("TRN2", target_bir_lowering=False, num_devices=1)
    arrays, args = {}, []
    for name in _INS:
        a = _np.ascontiguousarray(inputs[name])
        arrays[f"in_{name}_dram"] = a
        args.append(nc.dram_tensor(f"in_{name}_dram", a.shape, _mybir.dt.from_np(a.dtype), kind="ExternalInput").ap())
    for i, (shape, dtype) in enumerate(_OUTS):
        dt = _mybir.dt.from_np(_np.dtype(dtype))
        args.append(nc.dram_tensor(f"out_{i}_dram", shape, dt, kind="ExternalOutput").ap())
    adaln_block(nc, *args)
    r = _run(nc, [arrays], core_ids=[0])
    return r.results[0]["out_0_dram"]
```

```python
from contextlib import ExitStack

import concourse.bass as bass
from concourse import mybir

F32 = mybir.dt.float32
F32R = mybir.dt.float32r
ALU = mybir.AluOpType
ACT = mybir.ActivationFunctionType
AX_X = mybir.AxisListType.X
AX_XY = mybir.AxisListType.XY

P = 128
BANKS = 8
BANK = 512
EPS = 1e-5
GATE_FLOOR = 0.25


def bank_plan(NB, IC, NHG, NS):
    half, last = NB // 2, NS - 1
    uses = [("h_t", i, "a") for i in range(IC)]
    uses += [("wq_t", i, "v") for i in range(IC - 1)]
    uses += [("mod_attn", 0, "v"), ("wq_t", IC - 1, "v")]
    uses += [("q", j, "v") for j in range(half)]
    uses += [("h_t", IC + i, "a") for i in range(IC)]
    uses += [("wk_t", i, "v") for i in range(IC)]
    uses += [("q", j, "v") for j in range(half, NB)]
    uses += [("mod_ffn", 0, "v"), ("gate_attn", 0, "v"), ("gate_ffn", 0, "v")]
    uses += [("q_t", i, "a") for i in range(NHG)]
    uses += [("k", j, "v") for j in range(half)]
    uses += [("wv_t", i, "v") for i in range(IC)]
    uses += [("k", j, "v") for j in range(half, NB)]
    uses += [("k_t", i, "va"[i % 2]) for i in range(NHG)]
    uses += [("v", 0, "v"), ("v", 1, "v")]
    for s in range(NS):
        uses += [("scores", s, "a")]
        if s % 2 and s // 2 + 2 < NB:
            uses += [("v", s // 2 + 2, "v")]
        if s == last - 2:
            uses += [("v_t", i, "a") for i in range(NHG)]
    uses += [("as_t", 0, "a"), ("bs_t", 0, "a")]
    uses += [("b_t", i, "a") for i in range(IC)]
    uses += [("a_eff", i, "a") for i in range(IC // 2)]
    uses += [("ctx", s, "v") for s in range(NS)]
    uses += [("ctx_t", i, "v") for i in range(NHG)]
    uses += [("b_eff", i, "a") for i in range(2)]
    uses += [("h2_t", 0, "a")]
    for j in range(NB):
        if j + 1 < NB:
            uses += [("h2_t", j + 1, "a")]
        uses += [("ax", j, "a"), ("out", j, "v")]
    return uses


def adaln_block(nc, x, wq, bq, wk, bk, wv, bv, gate, kern, bias, lora_a, lora_b, lora_as, lora_bs, cond, wmod, out):
    tokens, hid = x.shape[1], x.shape[2]
    lora_n, rank = lora_a.shape[0], lora_a.shape[1]
    D = 16
    H = hid // D
    NB = tokens // P
    IC = hid // P
    HALF = 2
    SLOT = NB // HALF
    NHG = H // 4
    GB = BANK // (HALF * H)
    NS = P // GB
    NCH = NS // 2
    CH = 2 * BANK
    RCH = CH // H
    SCALE = float(D) ** -0.5
    W = IC * hid
    NBH = NB // 2
    assert NB == 8 and IC == 4 and H == 32 and gate.shape[0] == NB and lora_n * rank == hid and rank == 32
    NG = P // rank

    uses = bank_plan(NB, IC, NHG, NS)
    use_no = {(s, i): u for u, (s, i, _) in enumerate(uses)}

    with ExitStack() as ctx:
        def sb(name, cols):
            return ctx.enter_context(nc.sbuf_tensor(name, [P, cols], F32))

        def sem(name):
            return ctx.enter_context(nc.semaphore(name))

        KB = 1024
        area = -(-nc.sbuf_base // 32) * 32
        sb("area", 192 * KB // 4)

        def at(name, kb, cols, dt=F32):
            return nc.alloc_sbuf_tensor_at(name, [P, cols], dt, offset=area + kb * KB)[:]

        N = NB * hid
        xn = at("xn", 0, N)
        q_nat_r = at("q_nat", 16, N)
        h_full = at("h_full", 32, N)
        wq_nat_r = at("wq_nat", 48, W)
        wk_nat_r = at("wk_nat", 56, W)
        diag = at("diag", 0, SLOT * H * P)
        h2_hi = at("h2_hi", 0, N, F32R)
        h2_lo = at("h2_lo", 16, N, F32R)
        wm_attn_r = at("wm_attn", 64, 2 * W)
        wk_hi = at("wk_hi", 64, W, F32R)
        wk_lo = at("wk_lo", 72, W, F32R)
        wv_nat_r = at("wv_nat", 80, W)
        k2_r = at("k2", 64, HALF * H * P)
        p_t = at("p_t", 64, HALF * H * P)
        xn2_r = at("xn2", 64, N)
        h2_full = at("h2_full", 80, N)
        wm_rest_r = at("wm_rest", 96, 4 * W)
        qc = at("qc", 96, N)
        k_nat_r = at("k_nat", 112, N)
        sreg = at("s", 96, HALF * H * P)
        b_cat_r = at("b_cat", 96, N)
        kern_nat = at("kern_nat", 112, W)
        b_raw_r = at("b_raw", 120, 2 * hid)
        wA_hi = at("wA_hi", 128, W, F32R)
        wA_lo = at("wA_lo", 136, W, F32R)
        b_t_r = at("b_t", 128, W)
        a_cat_r = at("a_cat", 136, IC * NB * 2 * rank)
        xres = at("xres", 144, N)
        v_nat_r = at("v_nat", 144, N)
        hT_hi = at("hT_hi", 160, N, F32R)
        hT_lo = at("hT_lo", 176, N, F32R)
        v_c = at("v_c", 160, N)
        ctx_r = at("ctx_c", 160, N)
        la_nat_r = at("la_nat", 176, W)
        lb_nat_r = at("lb_nat", 184, W)
        kern_hi = at("kern_hi", 176, W, F32R)
        kern_lo = at("kern_lo", 184, W, F32R)

        bqk_bc = sb("bqk_bc", 2 * hid)
        bv_bc = sb("bv_bc", hid)
        ga_bc = sb("ga_bc", hid)
        gb_bc = sb("gb_bc", hid)
        bs_nat_r = sb("bs_nat", IC * rank)
        ident = sb("ident", P)
        ones = sb("ones", P)
        half_mask = sb("half_mask", HALF)
        d_mask = sb("d_mask", D)
        rank_mask = sb("rank_mask", rank)
        ga_col = sb("ga_col", H)
        gate_col = sb("gate_col", IC * NB)
        silu = sb("silu", 4 * IC)
        modc = sb("modc", 4 * IC)
        axT = sb("axT", 2 * P)
        stats = sb("stats", NB * 6)
        mv = sb("mv", NB * 2)
        std = sb("std", NB)
        rstd = sb("rstd", NB)
        rmax = sb("rmax", 2 * RCH)
        rsum = sb("rsum", 2 * RCH)
        rinv = sb("rinv", 2 * RCH)
        ps = ctx.enter_context(nc.psum_tensor("ps", [P, BANKS * BANK], F32))

        def chunked(reg):
            return reg.rearrange("p (c n) -> p c n", c=IC)

        x_v = xres.rearrange("p (j n) -> p j n", j=NB)
        x_hjd = xres.rearrange("p (j h d) -> p h j d", j=NB, d=D)
        xn_v = xn.rearrange("p (j n) -> p j n", j=NB)
        xn2 = xn2_r.rearrange("p (j n) -> p j n", j=NB)
        wm_attn = chunked(wm_attn_r)
        wm_rest = chunked(wm_rest_r)
        wq_nat, wk_nat, wv_nat = chunked(wq_nat_r), chunked(wk_nat_r), chunked(wv_nat_r)
        sign_tmp = wm_rest[:, 1, 0:hid]
        q_nat = q_nat_r.rearrange("p (h j d) -> p h j d", j=NB, d=D)
        k_nat = k_nat_r.rearrange("p (h j d) -> p h j d", j=NB, d=D)
        v_nat = v_nat_r.rearrange("p (f d s t) -> p f s t d", f=HALF, d=D, s=SLOT)
        k2 = k2_r.rearrange("p (f h g) -> p f h g", f=HALF, g=P)
        diag_s = diag.rearrange("p (s n) -> p s n", s=SLOT)
        diag_g = diag.rearrange("p (m g) -> p m g", g=P)
        k2_g = k2_r.rearrange("p (n g) -> p n g", g=P)
        pT_g = p_t.rearrange("p (g n) -> p g n", g=P)
        s_rows = sreg.rearrange("p (c r t) -> p c r t", c=NCH, t=H)
        ctx_c = ctx_r.rearrange("p (h g) -> p h g", g=P)
        ctx_w = ctx_r.rearrange("p (h g) -> p g h", g=P)
        h2F = h2_full.rearrange("p (j c t) -> p j c t", j=NB, c=IC)
        bq_bc, bk_bc = bqk_bc[:, 0:hid], bqk_bc[:, hid:2 * hid]
        gmix = bqk_bc[:].rearrange("p (c n) -> p c n", c=IC)
        la_nat, lb_nat = chunked(la_nat_r), chunked(lb_nat_r)
        as_nat = ga_bc
        b_tail = ga_bc
        bs_nat = bs_nat_r[:].rearrange("p (c r) -> p c r", c=IC)
        b_t = chunked(b_t_r)
        a_cat = a_cat_r.rearrange("p (c b r) -> p c b r", c=IC, b=NB)
        b_cat = b_cat_r.rearrange("p (b o) -> p b o", b=NB)
        b_raw = b_raw_r.rearrange("p (q o) -> p q o", q=2)

        psum_written = sem("psum_written")
        dve_emptied = sem("dve_emptied")
        act_emptied = sem("act_emptied")
        dve_chain = sem("dve_chain")
        pool_chain = sem("pool_chain")
        cond_in = sem("cond_in")
        wm_attn_in = sem("wm_attn_in")
        wm_rest_in = sem("wm_rest_in")
        x_in = [sem(f"x_in{j}") for j in range(NB)]
        wq_in = sem("wq_in")
        wk_in = sem("wk_in")
        wv_in = sem("wv_in")
        bqk_in = sem("bqk_in")
        bv_in = sem("bv_in")
        gate_in = sem("gate_in")
        kern_in = sem("kern_in")
        la_in = sem("la_in")
        lb_in = sem("lb_in")
        lsh_in = sem("lsh_in")
        bias_in = sem("bias_in")
        q_diag_in = sem("q_diag_in")
        v_diag_in = sem("v_diag_in")
        b_tail_in = sem("b_tail_in")
        b_eff_in = sem("b_eff_in")
        out_sent = sem("out_sent")
        ident_made = sem("ident_made")
        diag_zero = sem("diag_zero")
        w_hi_made = sem("w_hi_made")
        h_split = sem("h_split")
        mod_summed = sem("mod_summed")
        kern_hi_made = sem("kern_hi_made")
        kern_split = sem("kern_split")
        h2_hi_made = sem("h2_hi_made")
        h2_split = sem("h2_split")
        ones_row = sem("ones_row")
        ga_ready = sem("ga_ready")
        gates_ready = sem("gates_ready")
        x_again = sem("x_again")
        exp_c = sem("exp_c")
        var_ready = sem("var_ready")
        std_ready = sem("std_ready")
        xn_ready = sem("xn_ready")
        shifted = sem("shifted")
        exped = sem("exped")
        inv_ready = sem("inv_ready")
        normed = sem("normed")
        turned = sem("turned")
        ctx_gated = sem("ctx_gated")
        ctx_low = sem("ctx_low")
        gmix_made = sem("gmix_made")
        kern_scaled = sem("kern_scaled")
        b_scaled = sem("b_scaled")
        tail_scaled = sem("tail_scaled")
        ones_made = sem("ones_made")

        def bank(stage, i):
            b = use_no[stage, i] % BANKS
            return ps[:, b * BANK:(b + 1) * BANK]

        def written(stage, i):
            return use_no[stage, i] + 1

        def emptied(stage, i):
            u = use_no[stage, i]
            who = uses[u][2]
            return (dve_emptied if who == "v" else act_emptied), sum(1 for w in uses[:u + 1] if w[2] == who)

        block = ctx.enter_context(nc.Block())

        @block.sync
        def _(sp):
            sp.dma_start(silu[:, 0:IC], cond[0].rearrange("(c p) -> p c", p=P),
                         allow_slow_non_contiguous=True).then_inc(cond_in, 16)
            wm = wmod.rearrange("(c p) n -> p c n", p=P)
            xr = x[0].rearrange("(j p) n -> p j n", p=P)
            for j in range(NBH):
                sp.dma_start(x_v[:, j, :], xr[:, j, :]).then_inc(x_in[j], 16)
            sp.dma_start(wm_attn, wm[:, :, 0:2 * hid]).then_inc(wm_attn_in, 16)
            sp.dma_start(wq_nat, wq.rearrange("(c p) n -> p c n", p=P)).then_inc(wq_in, 16)
            for j in range(NBH, NB):
                sp.dma_start(x_v[:, j, :], xr[:, j, :]).then_inc(x_in[j], 16)
            sp.dma_start(bq_bc, bq.partition_broadcast(P)).then_inc(bqk_in, 16)
            sp.dma_start(bk_bc, bk.partition_broadcast(P)).then_inc(bqk_in, 16)
            sp.dma_start(wk_nat, wk.rearrange("(c p) n -> p c n", p=P)).then_inc(wk_in, 16)
            sp.dma_start(wm_rest, wm[:, :, 2 * hid:6 * hid]).then_inc(wm_rest_in, 16)
            sp.dma_start(wv_nat, wv.rearrange("(c p) n -> p c n", p=P)).then_inc(wv_in, 16)
            sp.dma_start(bv_bc[:], bv.partition_broadcast(P)).then_inc(bv_in, 16)
            sp.dma_start(bs_nat, lora_bs.rearrange("(c p) r -> p c r", p=P)).then_inc(lsh_in, 16)
            for n in range(NG):
                for c in range(IC):
                    sp.dma_start(gate_col[rank * n:rank * (n + 1), c * NB:(c + 1) * NB],
                                 gate[:, NG * c + n].partition_broadcast(rank),
                                 allow_slow_non_contiguous=True).then_inc(gate_in, 16)
            sp.wait_ge(ga_ready, 1)
            sp.dma_start(as_nat[0:rank, :], lora_as[:, :]).then_inc(lsh_in, 16)
            sp.dma_start(b_tail[2 * rank:2 * rank + 1, :], bias.rearrange("(a n) -> a n", a=1)).then_inc(bias_in, 16)
            sp.wait_ge(*emptied("q_t", NHG - 1))
            sp.wait_ge(diag_zero, 1)
            for s in range(SLOT):
                r = slice(32 * s, 32 * s + 32)
                sp.dma_start(diag_s[r, s, :], qc[r, :]).then_inc(q_diag_in, 16)
            sp.wait_ge(psum_written, written("v", NB - 1))
            for c in range(IC):
                sp.dma_start(lb_nat[:, c, :].rearrange("p (n r) -> p n r", r=rank),
                             lora_b[:, c * P:(c + 1) * P, :].rearrange("n p r -> p n r")).then_inc(lb_in, 16)
            sp.dma_start(la_nat, lora_a.rearrange("(c n) r i -> (n r) c i", n=NG)).then_inc(la_in, 16)
            sp.wait_ge(psum_written, written("scores", NS - 1))
            sp.wait_ge(*emptied("v_t", NHG - 1))
            for s in range(SLOT):
                r = slice(32 * s, 32 * s + 32)
                sp.dma_start(diag_s[r, s, :], v_c[r, :]).then_inc(v_diag_in, 16)
            sp.dma_start(xres.rearrange("p (j n) -> p j n", j=NB), xr).then_inc(x_again, 16)
            sp.wait_ge(turned, NCH)
            sp.dma_start(chunked(kern_nat), kern.rearrange("(c p) n -> p c n", p=P)).then_inc(kern_in, 16)
            sp.wait_ge(tail_scaled, 2)
            rows = slice(rank, 2 * rank)
            sp.dma_start(b_cat[rows], b_tail[rows, :].unsqueeze(1).to_broadcast([rank, NB, hid])).then_inc(b_tail_in, 16)
            rows = slice(2 * rank, 2 * rank + 1)
            sp.dma_start(b_cat[rows], b_tail[rows, :].unsqueeze(1).to_broadcast([1, NB, hid])).then_inc(b_tail_in, 16)
            sp.wait_ge(b_scaled, 1)
            for b in range(NB):
                r = slice(32 * (b % 4), 32 * (b % 4) + 32)
                sp.dma_start(b_cat[0:rank, b, :], b_raw[r, b // 4, :]).then_inc(b_eff_in, 16)
            orow = out[0].rearrange("(j p) n -> p j n", p=P)
            for j in range(NB):
                sp.wait_ge(*emptied("out", j))
                sp.dma_start(orow[:, j, :], x_v[:, j, :]).then_inc(out_sent, 16)
            sp.wait_ge(out_sent, 16 * NB)

        @block.gpsimd
        def _(pool):
            nc.gpsimd.memset(ident[:], 0.0).then_inc(pool_chain, 1)
            pool.wait_ge(pool_chain, 1)
            nc.gpsimd.affine_select(out=ident[:], in_=ident[:], compare_op=ALU.not_equal, fill=1.0, base=0,
                                    pattern=[[-1, P]], channel_multiplier=1).then_inc(ident_made, 1)
            nc.gpsimd.memset(ones[:], 1.0).then_inc(ones_made, 1)
            pool.wait_ge(psum_written, written("q_t", NHG - 1))
            pool.wait_ge(h_split, 2 * IC)
            nc.gpsimd.memset(diag, 0.0).then_inc(diag_zero, 1)
            pool.wait_ge(gate_in, 16 * NG * IC)
            pool.wait_ge(*emptied("k", NB - 1))
            nc.gpsimd.tensor_tensor(gmix.rearrange("p c (b r) -> p (c b) r", r=rank),
                                    gate_col[:].unsqueeze(2).to_broadcast([P, IC * NB, rank]),
                                    rank_mask[:].unsqueeze(1).to_broadcast([P, IC * NB, rank]),
                                    ALU.mult).then_inc(gmix_made, 1)
            for c in range(NCH):
                b = c % 2
                pool.wait_ge(inv_ready, c + 1)
                nc.gpsimd.tensor_tensor(s_rows[:, c], s_rows[:, c],
                                        rinv[:, b * RCH:(b + 1) * RCH].unsqueeze(2).to_broadcast([P, RCH, H]),
                                        ALU.mult).then_inc(normed, 1)
            pool.wait_ge(gates_ready, 1)
            pool.wait_ge(bias_in, 16)
            pool.wait_ge(normed, NCH)
            r = slice(2 * rank, 2 * rank + 1)
            nc.gpsimd.tensor_tensor(b_tail[r, :], b_tail[r, :], gb_bc[r, :], ALU.mult).then_inc(tail_scaled, 1)
            pool.wait_ge(*emptied("bs_t", 0))
            pool.wait_ge(tail_scaled, 1)
            r = slice(rank, 2 * rank)
            nc.gpsimd.tensor_tensor(b_tail[r, :], b_tail[r, :], gb_bc[r, :], ALU.mult).then_inc(tail_scaled, 1)
            pool.wait_ge(tail_scaled, 2)
            for s in range(0, NS, 2):
                if s == NS // 2:
                    pool.wait_ge(kern_in, 16)
                    nc.gpsimd.tensor_tensor(chunked(kern_nat), chunked(kern_nat),
                                            gb_bc[:].unsqueeze(1).to_broadcast([P, IC, hid]),
                                            ALU.mult).then_inc(kern_scaled, 1)
                pool.wait_ge(*emptied("ctx", s + 1))
                part = ctx_c[:, :, s * GB:(s + 2) * GB]
                nc.gpsimd.tensor_tensor(part, part, ga_col[:].unsqueeze(2).to_broadcast([P, H, 2 * GB]),
                                        ALU.mult).then_inc(ctx_gated, 1)
            pool.wait_ge(*emptied("b_eff", 1))
            nc.gpsimd.tensor_tensor(b_raw, b_raw, gb_bc[:].unsqueeze(1).to_broadcast([P, 2, hid]),
                                    ALU.mult).then_inc(b_scaled, 1)

        @block.scalar
        def _(act):
            def empty(stage, i, dst, src=None):
                act.wait_ge(psum_written, written(stage, i))
                nc.scalar.activation(dst, bank(stage, i) if src is None else src, ACT.Copy).then_inc(act_emptied, 1)

            act.wait_ge(cond_in, 16)
            nc.scalar.activation(silu[:, IC:2 * IC], silu[:, 0:IC], ACT.Exp, scale=-1.0).then_inc(exp_c, 1)

            def take_hi(stage, i, hi):
                act.wait_ge(psum_written, written(stage, i))
                nc.scalar.activation(hi[:, i * BANK:(i + 1) * BANK], bank(stage, i), ACT.Copy).then_inc(w_hi_made, 1)

            def deviations(k):
                act.wait_ge(var_ready, k + 1)
                k %= 2
                nc.scalar.activation(std[:, k * NBH:(k + 1) * NBH],
                                     mv[:].rearrange("p (j s) -> p j s", s=2)[:, k * NBH:(k + 1) * NBH, 1],
                                     ACT.Sqrt).then_inc(std_ready, 1)

            def h_t(k):
                for i in range(k * IC, (k + 1) * IC):
                    act.wait_ge(psum_written, written("h_t", i))
                    nc.scalar.activation(h_full[:, i * BANK:(i + 1) * BANK], bank("h_t", i), ACT.Identity,
                                         bias=modc[:, i % IC:i % IC + 1],
                                         scale=modc[:, IC + i % IC:IC + i % IC + 1]).then_inc(act_emptied, 1)

            deviations(0)
            for i in range(IC - 1):
                take_hi("wq_t", i, wA_hi)
            act.wait_ge(*emptied("mod_attn", 0))
            h_t(0)
            take_hi("wq_t", IC - 1, wA_hi)
            deviations(1)
            h_t(1)
            for i in range(IC):
                take_hi("wk_t", i, wk_hi)
            act.wait_ge(gates_ready, 1)
            for i in range(NHG):
                empty("q_t", i, qc[:, i * BANK:(i + 1) * BANK])
            for i in range(IC):
                take_hi("wv_t", i, wA_hi)
            for i in range(1, NHG, 2):
                act.wait_ge(psum_written, written("k_t", i))
                for f in range(HALF):
                    ins = nc.scalar.activation(k2[:, f, 4 * i:4 * i + 4, :],
                                               bank("k_t", i).rearrange("p (h g) -> p h g", g=P),
                                               ACT.Copy, scale=half_mask[:, f:f + 1])
                ins.then_inc(act_emptied, 1)

            def exp_chunk(c):
                act.wait_ge(shifted, c + 1)
                nc.scalar.activation(s_rows[:, c], s_rows[:, c], ACT.Exp, scale=SCALE).then_inc(exped, 1)

            act.wait_ge(q_diag_in, 16 * SLOT)
            for c in range(NCH):
                for s in (2 * c, 2 * c + 1):
                    empty("scores", s, sreg[:, s * BANK:(s + 1) * BANK])
                    if s == NS - 3:
                        for i in range(NHG):
                            empty("v_t", i, v_c[:, i * BANK:(i + 1) * BANK])
                if c:
                    exp_chunk(c - 1)
            exp_chunk(NCH - 1)
            act.wait_ge(psum_written, written("as_t", 0))
            nc.scalar.activation(a_cat[:, :, :, rank:2 * rank],
                                 bank("as_t", 0)[:, 0:IC * rank].rearrange("p (c r) -> p c r", c=IC)
                                 .unsqueeze(2).to_broadcast([P, IC, NB, rank]), ACT.Copy).then_inc(act_emptied, 1)
            empty("bs_t", 0, b_tail[rank:2 * rank, :], bank("bs_t", 0)[0:rank, :])
            for i in range(IC):
                empty("b_t", i, b_t[:, i, :])
            for i in range(IC // 2):
                empty("a_eff", i, a_cat[:, 2 * i:2 * i + 2, :, 0:rank],
                      bank("a_eff", i).rearrange("p (c b r) -> p c b r", c=2, b=NB))
            act.wait_ge(v_diag_in, 16 * SLOT)
            for s in range(NS):
                act.wait_ge(psum_written, written("ctx", s))
                nc.scalar.activation(ctx_w[:, s * GB:(s + 1) * GB, :],
                                     bank("ctx", s).rearrange("p (g f h) -> p g f h", f=HALF, h=H)[:, :, 0, :],
                                     ACT.Copy, scale=half_mask[:, 0:1]).then_inc(ctx_low, 1)
                if s == NS - 3:
                    act.wait_ge(kern_scaled, 1)
                    nc.scalar.activation(kern_hi, kern_nat, ACT.Copy).then_inc(kern_hi_made, 1)
            for i in range(2):
                empty("b_eff", i, b_raw[:, i, :])

            def h2_t(j):
                act.wait_ge(psum_written, written("h2_t", j))
                for c in range(IC):
                    ins = nc.scalar.activation(h2F[:, j, c, :], bank("h2_t", j)[:, c * P:(c + 1) * P], ACT.Identity,
                                               bias=modc[:, 2 * IC + c:2 * IC + c + 1],
                                               scale=modc[:, 3 * IC + c:3 * IC + c + 1])
                ins.then_inc(act_emptied, 1)
                act.wait_ge(*emptied("h2_t", j))
                nc.scalar.activation(h2_hi[:, j * hid:(j + 1) * hid], h2_full[:, j * hid:(j + 1) * hid],
                                     ACT.Copy).then_inc(h2_hi_made, 1)

            deviations(2)
            deviations(3)
            act.wait_ge(*emptied("mod_ffn", 0))
            h2_t(0)
            for j in range(NB):
                if j + 1 < NB:
                    h2_t(j + 1)
                if j >= 2:
                    act.wait_ge(psum_written, written("out", j - 2))
                empty("ax", j, axT[0:2 * rank, (j % 2) * P:(j % 2 + 1) * P], bank("ax", j)[0:2 * rank, 0:P])

        @block.vector
        def _(dve):
            chain = [0]

            def link(ins):
                chain[0] += 1
                ins.then_inc(dve_chain, 1)
                dve.wait_ge(dve_chain, chain[0])

            mv_v = mv[:].rearrange("p (j s) -> p j s", s=2)

            nc.vector.memset(axT[2 * rank:2 * rank + 1, :], 1.0).then_inc(ones_row, 1)
            dve.wait_ge(exp_c, 1)
            link(nc.vector.tensor_scalar(silu[:, 2 * IC:3 * IC], silu[:, IC:2 * IC], 1.0, None, ALU.add))
            link(nc.vector.reciprocal(silu[:, 3 * IC:4 * IC], silu[:, 2 * IC:3 * IC]))
            link(nc.vector.tensor_tensor(silu[:, 2 * IC:3 * IC], silu[:, 0:IC], silu[:, 3 * IC:4 * IC], ALU.mult))
            dve.wait_ge(ident_made, 1)
            nc.vector.tensor_reduce(half_mask[:], ident[:].rearrange("p (s f d) -> p f s d", f=HALF, d=D), AX_XY, ALU.add)
            nc.vector.tensor_reduce(d_mask[:], ident[:].rearrange("p (j d) -> p d j", d=D), AX_X, ALU.add)
            link(nc.vector.tensor_reduce(rank_mask[:], ident[:].rearrange("p (n r) -> p r n", r=rank), AX_X, ALU.add))

            def layer_norm_stats(j0, j1):
                for j in range(j0, j1):
                    ins = nc.vector.bn_stats(stats[:, 6 * j:6 * j + 6], x_v[:, j, :])
                link(ins)
                for j in range(j0, j1):
                    ins = nc.vector.bn_aggr(mv_v[:, j, :], stats[:, 6 * j:6 * j + 6])
                link(ins)
                nc.vector.tensor_scalar(mv_v[:, j0:j1, 1], mv_v[:, j0:j1, 1], EPS, None, ALU.add).then_inc(var_ready, 1)

            def normalise(k, dst):
                j0, j1 = (k % 2) * NBH, (k % 2 + 1) * NBH
                dve.wait_ge(std_ready, k + 1)
                link(nc.vector.reciprocal(rstd[:, j0:j1], std[:, j0:j1]))
                for j in range(j0, j1):
                    nc.vector.tensor_scalar(dst[:, j, :], x_v[:, j, :], mv_v[:, j, 0:1], rstd[:, j:j + 1],
                                            ALU.subtract, ALU.mult).then_inc(xn_ready, 1)

            def modulation(w, k):
                link(nc.vector.tensor_scalar(w[:, 0], w[:, 0], silu[:, 2 * IC:2 * IC + 1], None, ALU.mult))
                for c in range(1, IC):
                    ins = nc.vector.scalar_tensor_tensor(out=w[:, 0], in0=w[:, c],
                                                         scalar=silu[:, 2 * IC + c:2 * IC + c + 1], in1=w[:, 0],
                                                         op0=ALU.mult, op1=ALU.add)
                    if c + 1 < IC:
                        link(ins)
                ins.then_inc(mod_summed, 1)

            def mod_columns(stage, o0):
                dve.wait_ge(psum_written, written(stage, 0))
                nc.vector.tensor_copy(modc[:, o0:o0 + IC], bank(stage, 0)[:, 0:IC])
                nc.vector.tensor_scalar(modc[:, o0 + IC:o0 + 2 * IC], bank(stage, 0)[:, IC:2 * IC], 1.0, None,
                                        ALU.add).then_inc(dve_emptied, 1)

            weights_taken = [0]

            def take_lo(stage, i, hi, lo):
                weights_taken[0] += 1
                dve.wait_ge(w_hi_made, weights_taken[0])
                c = slice(i * BANK, (i + 1) * BANK)
                nc.vector.tensor_tensor(lo[:, c], bank(stage, i), hi[:, c].bitcast(F32),
                                        ALU.subtract).then_inc(dve_emptied, 1)

            def split_h(k):
                for i in range(k * IC, (k + 1) * IC):
                    src = h_full[:, i * BANK:(i + 1) * BANK]
                    c = slice((i % IC) * tokens + k * BANK, (i % IC) * tokens + (k + 1) * BANK)
                    dve.wait_ge(*emptied("h_t", i))
                    link(nc.vector.tensor_copy(hT_hi[:, c], src))
                    nc.vector.tensor_tensor(hT_lo[:, c], src, hT_hi[:, c].bitcast(F32),
                                            ALU.subtract).then_inc(h_split, 1)

            def take_q(j):
                dve.wait_ge(psum_written, written("q", j))
                nc.vector.tensor_tensor(q_nat[:, :, j, :], bank("q", j).rearrange("p (h d) -> p h d", d=D),
                                        bq_bc.rearrange("p (h d) -> p h d", d=D), ALU.add).then_inc(dve_emptied, 1)

            for j in range(NBH):
                dve.wait_ge(x_in[j], 16)
            layer_norm_stats(0, NBH)
            normalise(0, xn_v)
            dve.wait_ge(wm_attn_in, 16)
            modulation(wm_attn, 0)
            for i in range(IC - 1):
                take_lo("wq_t", i, wA_hi, wA_lo)
            mod_columns("mod_attn", 0)
            split_h(0)
            take_lo("wq_t", IC - 1, wA_hi, wA_lo)
            for j in range(NBH, NB):
                dve.wait_ge(x_in[j], 16)
            layer_norm_stats(NBH, NB)
            normalise(1, xn_v)
            dve.wait_ge(bqk_in, 32)
            for j in range(NBH):
                take_q(j)
            split_h(1)
            for i in range(IC):
                take_lo("wk_t", i, wk_hi, wk_lo)
            dve.wait_ge(wm_rest_in, 16)
            modulation(wm_rest, 1)
            for j in range(NBH, NB):
                take_q(j)
            mod_columns("mod_ffn", 2 * IC)
            for name, dst in (("gate_attn", ga_bc), ("gate_ffn", gb_bc)):
                dve.wait_ge(psum_written, written(name, 0))
                link(nc.vector.tensor_scalar(sign_tmp, bank(name, 0), 0.0, 2.0, ALU.is_ge, ALU.mult))
                nc.vector.scalar_tensor_tensor(out=dst[:], in0=sign_tmp, scalar=-1.0, in1=bank(name, 0),
                                               op0=ALU.add, op1=ALU.mult).then_inc(dve_emptied, 1)
                dve.wait_ge(*emptied(name, 0))
                link(nc.vector.tensor_scalar(dst[:], dst[:], GATE_FLOOR, None, ALU.max))
                ins = nc.vector.scalar_tensor_tensor(out=dst[:], in0=sign_tmp, scalar=-1.0, in1=dst[:],
                                                     op0=ALU.add, op1=ALU.mult)
                if name == "gate_attn":
                    link(ins)
                    link(nc.vector.tensor_tensor(sign_tmp.rearrange("p (h d) -> p h d", d=D),
                                                 ga_bc[:].rearrange("p (h d) -> p h d", d=D),
                                                 d_mask[:].unsqueeze(1).to_broadcast([P, H, D]), ALU.mult))
                    ins = nc.vector.tensor_reduce(ga_col[:], sign_tmp.rearrange("p (h d) -> p h d", d=D), AX_X,
                                                  ALU.add)
                    ins.then_inc(ga_ready, 1)
                    dve.wait_ge(ga_ready, 1)
                else:
                    ins.then_inc(gates_ready, 1)
            for j in range(NB):
                if j == NBH:
                    for i in range(IC):
                        take_lo("wv_t", i, wA_hi, wA_lo)
                dve.wait_ge(psum_written, written("k", j))
                nc.vector.tensor_tensor(k_nat[:, :, j, :], bank("k", j).rearrange("p (h d) -> p h d", d=D),
                                        bk_bc.rearrange("p (h d) -> p h d", d=D), ALU.add).then_inc(dve_emptied, 1)
            for i in range(0, NHG, 2):
                dve.wait_ge(psum_written, written("k_t", i))
                for f in range(HALF):
                    ins = nc.vector.tensor_scalar(k2[:, f, 4 * i:4 * i + 4, :],
                                                  bank("k_t", i).rearrange("p (h g) -> p h g", g=P),
                                                  half_mask[:, f:f + 1], None, ALU.mult)
                ins.then_inc(dve_emptied, 1)

            def take_v(j):
                dve.wait_ge(psum_written, written("v", j))
                nc.vector.tensor_tensor(v_nat[:, j % HALF, j // HALF], bank("v", j).rearrange("p (h d) -> p h d", d=D),
                                        bv_bc[:].rearrange("p (h d) -> p h d", d=D), ALU.add).then_inc(dve_emptied, 1)

            def row_max(c):
                b = c % 2
                dve.wait_ge(*emptied("scores", 2 * c + 1))
                m = rmax[:, b * RCH:(b + 1) * RCH]
                link(nc.vector.tensor_reduce(m, s_rows[:, c], AX_X, ALU.max))
                nc.vector.tensor_tensor(s_rows[:, c], s_rows[:, c], m.unsqueeze(2).to_broadcast([P, RCH, H]),
                                        ALU.subtract).then_inc(shifted, 1)

            def row_sum(c):
                b = c % 2
                dve.wait_ge(exped, c + 1)
                link(nc.vector.tensor_reduce(rsum[:, b * RCH:(b + 1) * RCH], s_rows[:, c], AX_X, ALU.add))
                if c >= 2:
                    dve.wait_ge(normed, c - 1)
                nc.vector.reciprocal(rinv[:, b * RCH:(b + 1) * RCH], rsum[:, b * RCH:(b + 1) * RCH]).then_inc(inv_ready, 1)

            dve.wait_ge(bv_in, 16)
            take_v(0)
            take_v(1)
            for c in range(NCH):
                if c + 2 < NB:
                    take_v(c + 2)
                row_max(c)
                if c:
                    row_sum(c - 1)

            def turn(c):
                dve.wait_ge(normed, c + 1)
                nc.vector.transpose(p_t[:, c * CH:(c + 1) * CH], sreg[:, c * CH:(c + 1) * CH]).then_inc(turned, 1)

            dve.wait_ge(psum_written, written("scores", NS - 1))
            turn(0)
            row_sum(NCH - 1)
            for c in range(1, NCH):
                turn(c)
            for s in range(NS):
                dve.wait_ge(ctx_low, s + 1)
                dst = ctx_w[:, s * GB:(s + 1) * GB, :]
                nc.vector.scalar_tensor_tensor(
                    out=dst, in0=bank("ctx", s).rearrange("p (g f h) -> p g f h", f=HALF, h=H)[:, :, 1, :],
                    scalar=half_mask[:, 1:2], in1=dst, op0=ALU.mult, op1=ALU.add).then_inc(dve_emptied, 1)
                if s == NS - 3:
                    dve.wait_ge(kern_hi_made, 1)
                    nc.vector.tensor_tensor(kern_lo, kern_nat, kern_hi.bitcast(F32),
                                            ALU.subtract).then_inc(kern_split, 1)
            dve.wait_ge(x_again, 16)
            for i in range(NHG):
                dve.wait_ge(psum_written, written("ctx_t", i))
                dst = x_hjd[:, 4 * i:4 * i + 4]
                nc.vector.tensor_tensor(dst, bank("ctx_t", i).rearrange("p (h j d) -> p h j d", h=4, d=D), dst,
                                        ALU.add).then_inc(dve_emptied, 1)
            dve.wait_ge(*emptied("ctx_t", NHG - 1))
            layer_norm_stats(0, NBH)
            layer_norm_stats(NBH, NB)
            normalise(2, xn2)
            normalise(3, xn2)

            def split_h2(j):
                c = slice(j * hid, (j + 1) * hid)
                dve.wait_ge(h2_hi_made, j + 1)
                nc.vector.tensor_tensor(h2_lo[:, c], h2_full[:, c], h2_hi[:, c].bitcast(F32),
                                        ALU.subtract).then_inc(h2_split, 1)

            split_h2(0)
            for j in range(NB):
                if j + 1 < NB:
                    split_h2(j + 1)
                dve.wait_ge(psum_written, written("out", j))
                nc.vector.tensor_tensor(x_v[:, j, :], bank("out", j), x_v[:, j, :], ALU.add).then_inc(dve_emptied, 1)

        @block.tensor
        def _(pe):
            def take(stage, i):
                u = use_no[stage, i]
                if u >= BANKS:
                    pe.wait_ge(*emptied(*uses[u - BANKS][0:2]))
                return bank(stage, i)

            def mod_columns(stage, w, cols):
                dst = take(stage, 0)
                for n, o0 in enumerate(cols):
                    ins = nc.tensor.matmul(dst[:, n:n + 1], w[:, 0, o0:o0 + P], ones[:, 0:1], start=True, stop=True)
                ins.then_inc(psum_written, 1)

            def gate_rows(stage, o0):
                nc.tensor.matmul(take(stage, 0), ones[:], wm_rest[:, 0, o0:o0 + hid],
                                 start=True, stop=True).then_inc(psum_written, 1)

            def transposes(stage, i, blocks):
                dst = take(stage, i)
                for n, src in enumerate(blocks):
                    k, m = src.shape[0], src.shape[1]
                    ins = nc.tensor.transpose(dst[0:m, n * k:(n + 1) * k], src, ident[0:k, 0:k])
                ins.then_inc(psum_written, 1)

            def weight_t(stage, w_nat, chunks):
                for i in chunks:
                    transposes(stage, i, [w_nat[:, c, i * P:(i + 1) * P] for c in range(IC)])

            def split_product(dst, a_hi, a_lo, b_hi, b_lo, start, stop):
                nc.tensor.matmul(dst, a_hi, b_lo, start=start, stop=False)
                nc.tensor.matmul(dst, a_lo, b_hi, start=False, stop=False)
                return nc.tensor.matmul(dst, a_hi, b_hi, start=False, stop=stop)

            def project(stage, j, w_hi, w_lo):
                dst = take(stage, j)
                for c in range(IC):
                    t, o = slice(c * tokens + j * P, c * tokens + (j + 1) * P), slice(c * hid, (c + 1) * hid)
                    ins = split_product(dst, hT_hi[:, t], hT_lo[:, t], w_hi[:, o], w_lo[:, o], c == 0, c == IC - 1)
                ins.then_inc(psum_written, 1)

            def h_t(k):
                pe.wait_ge(xn_ready, (k + 1) * NBH)
                for i in range(IC):
                    transposes("h_t", k * IC + i,
                               [xn_v[:, j, i * P:(i + 1) * P] for j in range(k * NBH, (k + 1) * NBH)])

            pe.wait_ge(ident_made, 1)
            h_t(0)
            pe.wait_ge(wq_in, 16)
            weight_t("wq_t", wq_nat, range(IC - 1))
            pe.wait_ge(ones_made, 1)
            pe.wait_ge(mod_summed, 1)
            mod_columns("mod_attn", wm_attn, [c * P for c in range(2 * IC)])
            weight_t("wq_t", wq_nat, [IC - 1])
            pe.wait_ge(h_split, IC)
            pe.wait_ge(*emptied("wq_t", IC - 1))
            for j in range(NBH):
                project("q", j, wA_hi, wA_lo)
            h_t(1)
            pe.wait_ge(wk_in, 16)
            weight_t("wk_t", wk_nat, range(IC))
            pe.wait_ge(h_split, 2 * IC)
            for j in range(NBH, NB):
                project("q", j, wA_hi, wA_lo)
            pe.wait_ge(mod_summed, 2)
            mod_columns("mod_ffn", wm_rest, [hid + c * P for c in range(2 * IC)])
            gate_rows("gate_attn", 0)
            gate_rows("gate_ffn", 3 * hid)
            pe.wait_ge(*emptied("q", NB - 1))
            for i in range(NHG):
                transposes("q_t", i, [q_nat_r[:, h * P:(h + 1) * P] for h in range(4 * i, 4 * i + 4)])
            pe.wait_ge(*emptied("wk_t", IC - 1))
            for j in range(NB):
                if j == NBH:
                    pe.wait_ge(wv_in, 16)
                    weight_t("wv_t", wv_nat, range(IC))
                project("k", j, wk_hi, wk_lo)
            pe.wait_ge(*emptied("k", NB - 1))
            for i in range(NHG):
                transposes("k_t", i, [k_nat_r[:, h * P:(h + 1) * P] for h in range(4 * i, 4 * i + 4)])
            pe.wait_ge(*emptied("wv_t", IC - 1))
            project("v", 0, wA_hi, wA_lo)
            project("v", 1, wA_hi, wA_lo)
            pe.wait_ge(q_diag_in, 16 * SLOT)
            pe.wait_ge(*emptied("k_t", NHG - 2))
            pe.wait_ge(*emptied("k_t", NHG - 1))
            for s in range(NS):
                dst = take("scores", s)
                for n in range(GB):
                    g = s * GB + n
                    ins = nc.tensor.matmul(dst[:, n * HALF * H:(n + 1) * HALF * H], diag_g[:, :, g], k2_g[:, :, g],
                                           start=True, stop=True)
                ins.then_inc(psum_written, 1)
                if s % 2 and s // 2 + 2 < NB:
                    project("v", s // 2 + 2, wA_hi, wA_lo)
                if s == NS - 3:
                    pe.wait_ge(*emptied("v", NB - 1))
                    for i in range(NHG):
                        transposes("v_t", i, [v_nat_r[:, n * P:(n + 1) * P] for n in range(4 * i, 4 * i + 4)])

            pe.wait_ge(lsh_in, 32)
            transposes("as_t", 0, [as_nat[0:rank, c * P:(c + 1) * P] for c in range(IC)])
            transposes("bs_t", 0, [bs_nat[:, c, :] for c in range(IC)])
            pe.wait_ge(lb_in, 16 * IC)
            weight_t("b_t", lb_nat, range(IC))
            pe.wait_ge(la_in, 16)
            pe.wait_ge(gmix_made, 1)
            for i in range(IC // 2):
                dst = take("a_eff", i)
                for n in range(2):
                    ic = 2 * i + n
                    for c in range(IC):
                        ins = nc.tensor.matmul(dst[:, n * NB * rank:(n + 1) * NB * rank],
                                               la_nat[:, c, ic * P:(ic + 1) * P], gmix[:, c, :],
                                               start=(c == 0), stop=(c == IC - 1))
                ins.then_inc(psum_written, 1)

            pe.wait_ge(v_diag_in, 16 * SLOT)
            for s in range(NS):
                if s % 2 == 0:
                    pe.wait_ge(turned, s // 2 + 1)
                dst = take("ctx", s)
                for n in range(GB):
                    g = s * GB + n
                    ins = nc.tensor.matmul(dst[:, n * HALF * H:(n + 1) * HALF * H], diag_g[:, :, g], pT_g[:, g, :],
                                           start=True, stop=True)
                ins.then_inc(psum_written, 1)
            pe.wait_ge(ctx_gated, NS // 2)
            for i in range(NHG):
                transposes("ctx_t", i, [ctx_c[:, h, :] for h in range(4 * i, 4 * i + 4)])

            pe.wait_ge(*emptied("b_t", IC - 1))
            for i in range(2):
                dst = take("b_eff", i)
                for c in range(IC):
                    ins = nc.tensor.matmul(dst, gmix[:, c, i * P:(i + 1) * P], b_t[:, c, :],
                                           start=(c == 0), stop=(c == IC - 1))
                ins.then_inc(psum_written, 1)

            def h2_t(j):
                pe.wait_ge(xn_ready, NB + j + 1)
                transposes("h2_t", j, [xn2[:, j, c * P:(c + 1) * P] for c in range(IC)])

            h2_t(0)
            for j in range(NB):
                if j + 1 < NB:
                    h2_t(j + 1)
                pe.wait_ge(*emptied("h2_t", j))
                if j == 0:
                    pe.wait_ge(*emptied("a_eff", IC // 2 - 1))
                dst = take("ax", j)[0:2 * rank, 0:P]
                for c in range(IC):
                    ins = nc.tensor.matmul(dst, a_cat[:, c, j, :], h2F[:, j, c, :], start=(c == 0), stop=(c == IC - 1))
                ins.then_inc(psum_written, 1)
                if j == 0:
                    pe.wait_ge(kern_split, 1)
                pe.wait_ge(h2_split, j + 1)
                dst = take("out", j)
                for c in range(IC):
                    t, o = slice(j * hid + c * P, j * hid + (c + 1) * P), slice(c * hid, (c + 1) * hid)
                    split_product(dst, h2_hi[:, t], h2_lo[:, t], kern_hi[:, o], kern_lo[:, o], c == 0, False)
                if j == 0:
                    pe.wait_ge(ones_row, 1)
                    pe.wait_ge(b_tail_in, 32)
                    pe.wait_ge(b_eff_in, 16 * NB)
                pe.wait_ge(*emptied("ax", j))
                rows = 2 * rank + 1
                nc.tensor.matmul(dst, axT[0:rows, (j % 2) * P:(j % 2 + 1) * P], b_cat[0:rows, j, :],
                                 start=False, stop=True).then_inc(psum_written, 1)


_INS = ["L0_attn_hidden_states", "L0_attn_wq", "L0_attn_bq", "L0_attn_wk", "L0_attn_bk", "L0_attn_wv", "L0_attn_bv",
        "L0_ffn_gate", "L0_ffn_kernel", "L0_ffn_bias", "L0_ffn_lora_A", "L0_ffn_lora_B", "L0_ffn_lora_A_shared",
        "L0_ffn_lora_B_shared", "L0_c", "L0_wmod"]
_OUTS = [((1, 1024, 512), "float32")]


def kernel(**inputs):
    import numpy as _np
    import concourse.bacc as _bacc
    from concourse import mybir as _mybir
    from concourse.bass_utils import run_bass_kernel_spmd as _run

    nc = _bacc.Bacc("TRN2", target_bir_lowering=False, num_devices=1)
    arrays, args = {}, []
    for name in _INS:
        a = _np.ascontiguousarray(inputs[name])
        arrays[f"in_{name}_dram"] = a
        args.append(nc.dram_tensor(f"in_{name}_dram", a.shape, _mybir.dt.from_np(a.dtype), kind="ExternalInput").ap())
    for i, (shape, dtype) in enumerate(_OUTS):
        dt = _mybir.dt.from_np(_np.dtype(dtype))
        args.append(nc.dram_tensor(f"out_{i}_dram", shape, dt, kind="ExternalOutput").ap())
    adaln_block(nc, *args)
    r = _run(nc, [arrays], core_ids=[0])
    return r.results[0]["out_0_dram"]
```

```python
from contextlib import ExitStack

from concourse import mybir

F32 = mybir.dt.float32
F32R = mybir.dt.float32r
ALU = mybir.AluOpType
ACT = mybir.ActivationFunctionType
AX_X = mybir.AxisListType.X
AX_XY = mybir.AxisListType.XY

P = 128
BANKS = 8
BANK = 512
EPS = 1e-5
V_FIRST = 3
GATE_FLOOR = 0.25


def out_parts(NB, hid):
    parts = [(j, slice(0, hid)) for j in range(NB - 1)]
    return parts + [(NB - 1, slice(0, hid // 2)), (NB - 1, slice(hid // 2, hid))]


def bank_plan(NB, IC, NHG, NS):
    uses = [("h_t", i, "a") for i in range(IC)]
    uses += [("mod_attn", i, "v") for i in range(2)]
    uses += [("wq_t", i, "v") for i in range(IC)]
    uses += [("h_t", IC + i, "a") for i in range(IC)]
    uses += [("q", i, "a") for i in range(IC)]
    uses += [("wk_t", i, "v") for i in range(IC)]
    uses += [("q", IC + i, "a") for i in range(IC)]
    uses += [("wv_t", i, "v") for i in range(IC)]
    uses += [("k", i, "a") for i in range(2)]
    uses += [("mod_ffn", 0, "v"), ("gate_attn", 0, "v"), ("gate_ffn", 0, "v")]
    uses += [("k", i, "a") for i in range(2, 2 * IC)]
    uses += [("v", i, "a") for i in range(V_FIRST)]
    for s in range(NS):
        uses += [("scores", s, "a")]
        if s % 2 and s // 2 + V_FIRST < 2 * IC:
            uses += [("v", s // 2 + V_FIRST, "a")]
    uses += [("as_t", 0, "a"), ("bs_t", 0, "a")]
    uses += [("b_t", i, "a") for i in range(IC)]
    uses += [("a_eff", i, "a") for i in range(IC - 1)]
    uses += [("ctx", s, "v") for s in range(NS)]
    uses += [("a_eff", IC - 1, "a")]
    uses += [("ctx_t", i, "v") for i in range(NHG)]
    uses += [("b_eff", 0, "a"), ("h2_t", 0, "a"), ("h2_t", 1, "a")]
    for j in range(NB):
        if 0 < j < NB - 1:
            uses += [("h2_t", j + 1, "a")]
        uses += [("ax", j, "v")]
        if j == 0:
            uses += [("b_eff", 1, "a")]
        uses += [("out", j, "v")]
    uses += [("out", NB, "v")]
    return uses


def adaln_block(nc, x, wq, bq, wk, bk, wv, bv, gate, kern, bias, lora_a, lora_b, lora_as, lora_bs, cond, wmod, out):
    tokens, hid = x.shape[1], x.shape[2]
    lora_n, rank = lora_a.shape[0], lora_a.shape[1]
    D = 16
    H = hid // D
    NB = tokens // P
    IC = hid // P
    HALF = 2
    SLOT = NB // HALF
    NHG = H // 4
    GB = BANK // (HALF * H)
    NS = P // GB
    NCH = NS // 2
    CH = 2 * BANK
    RCH = CH // H
    SCALE = float(D) ** -0.5
    W = IC * hid
    NBH = NB // 2
    XN_ACT = range(NB // 4, NBH)
    XN_DVE = NB - len(XN_ACT)
    KERN_AT = NS // 2 - 2
    assert NB == 8 and IC == 4 and H == 32 and gate.shape[0] == NB and lora_n * rank == hid and rank == 32
    NG = P // rank

    uses = bank_plan(NB, IC, NHG, NS)
    parts = out_parts(NB, hid)
    use_no = {(s, i): u for u, (s, i, _) in enumerate(uses)}

    with ExitStack() as ctx:
        def sb(name, cols, dt=F32):
            return ctx.enter_context(nc.sbuf_tensor(name, [P, cols], dt))

        def sem(name):
            return ctx.enter_context(nc.semaphore(name))

        KB = 1024
        area = -(-nc.sbuf_base // 32) * 32
        sb("area", 192 * KB // 4)

        def at(name, kb, cols, dt=F32):
            return nc.alloc_sbuf_tensor_at(name, [P, cols], dt, offset=area + kb * KB)[:]

        N = NB * hid
        x_r = at("x", 0, N)
        h_full = at("h_full", 16, N)
        wm_attn_r = at("wm_attn", 32, 2 * W)
        wq_nat_r = at("wq_nat", 48, W)
        diag = at("diag", 0, SLOT * H * P)
        h2_hi = at("h2_hi", 0, N, F32R)
        h2_lo = at("h2_lo", 16, N, F32R)
        b_hi_r = at("b_hi", 32, N, F32R)
        b_lo_r = at("b_lo", 48, N, F32R)
        q_r = at("q", 64, N)
        wk_nat_r = at("wk_nat", 80, W)
        wv_nat_r = at("wv_nat", 88, W)
        k2_r = at("k2", 64, HALF * H * P)
        p_t = at("p_t", 64, HALF * H * P)
        xn2_r = at("xn2", 64, N)
        h2_full = at("h2_full", 80, N)
        wm_rest_r = at("wm_rest", 96, 4 * W)
        k_r = at("k", 112, N)
        sreg = at("s", 96, HALF * H * P)
        b_cat_r = at("b_cat", 96, N)
        kern_nat = at("kern_nat", 112, W)
        kern_hi = at("kern_hi", 120, W, F32R)
        wA_hi = at("wA_hi", 128, W, F32R)
        wA_lo = at("wA_lo", 136, W, F32R)
        b_t_r = at("b_t", 128, W)
        a_cat_r = at("a_cat", 136, IC * NB * 2 * rank)
        wk_hi = at("wk_hi", 144, W, F32R)
        wk_lo = at("wk_lo", 152, W, F32R)
        v_r = at("v", 144, N)
        xres = at("xres", 144, N)
        hT_hi = at("hT_hi", 160, N, F32R)
        hT_lo = at("hT_lo", 176, N, F32R)
        ctx_r = at("ctx_c", 160, N)
        la_nat_r = at("la_nat", 176, W)
        lb_nat_r = at("lb_nat", 184, W)
        b_raw_r = at("b_raw", 176, 2 * hid)
        kern_lo = at("kern_lo", 184, W, F32R)

        gmix_r = sb("gmix", IC * NB // NG * P)
        b_col = sb("b_col", 3 * IC)
        ga_bc = sb("ga_bc", hid)
        gb_bc = sb("gb_bc", hid)
        bs_nat_r = sb("bs_nat", IC * rank)
        ident = sb("ident", P)
        ones = sb("ones", P)
        half_mask = sb("half_mask", HALF)
        d_mask = sb("d_mask", D)
        rank_mask = sb("rank_mask", rank)
        ga_col = sb("ga_col", H)
        gate_col = sb("gate_col", IC * NB)
        silu = sb("silu", 4 * IC)
        modc = sb("modc", 4 * IC)
        ax_parts = sb("ax_parts", 2 * P, F32R)
        bias_bc = sb("bias_bc", hid)
        stats = sb("stats", NB * 6)
        mv = sb("mv", NB * 2)
        std = sb("std", NB)
        rstd = sb("rstd", NB)
        shift = sb("shift", NB // 4)
        rmax = sb("rmax", 2 * RCH)
        rsum = sb("rsum", 2 * RCH)
        rinv = sb("rinv", 2 * RCH)
        ps = ctx.enter_context(nc.psum_tensor("ps", [P, BANKS * BANK], F32))

        def chunked(reg):
            return reg.rearrange("p (c n) -> p c n", c=IC)

        x_v = xres.rearrange("p (j n) -> p j n", j=NB)
        x_hjd = xres.rearrange("p (j h d) -> p h j d", j=NB, d=D)
        xn_v = x_r.rearrange("p (j n) -> p j n", j=NB)
        xn2 = xn2_r.rearrange("p (j n) -> p j n", j=NB)
        wm_attn = chunked(wm_attn_r)
        wm_rest = chunked(wm_rest_r)
        wq_nat, wk_nat, wv_nat = chunked(wq_nat_r), chunked(wk_nat_r), chunked(wv_nat_r)
        sign_tmp = wm_rest[:, 1, 0:hid]
        q_c, k_c, v_c = (t.rearrange("p (c n) -> p c n", c=IC) for t in (q_r, k_r, v_r))
        k2_j = k2_r.rearrange("p (f n) -> p f n", f=HALF)
        diag_s = diag.rearrange("p (s n) -> p s n", s=SLOT)
        diag_g = diag.rearrange("p (m g) -> p m g", g=P)
        k2_g = k2_r.rearrange("p (n g) -> p n g", g=P)
        pT_g = p_t.rearrange("p (g n) -> p g n", g=P)
        s_rows = sreg.rearrange("p (c r t) -> p c r t", c=NCH, t=H)
        ctx_c = ctx_r.rearrange("p (h g) -> p h g", g=P)
        ctx_w = ctx_r.rearrange("p (h g) -> p g h", g=P)
        h2F = h2_full.rearrange("p (j c t) -> p j c t", j=NB, c=IC)
        gmix = gmix_r[:].rearrange("p (c n) -> p c n", c=IC)
        la_nat, lb_nat = chunked(la_nat_r), chunked(lb_nat_r)
        as_nat = ga_bc
        b_tail = ga_bc
        bs_nat = bs_nat_r[:].rearrange("p (c r) -> p c r", c=IC)
        b_t = chunked(b_t_r)
        a_cat = a_cat_r.rearrange("p (c b r) -> p c b r", c=IC, b=NB)
        b_cat, b_hi, b_lo = (t.rearrange("p (b o) -> p b o", b=NB)
                             for t in (b_cat_r, b_hi_r, b_lo_r))
        b_raw = b_raw_r.rearrange("p (q o) -> p q o", q=2)

        psum_written = sem("psum_written")
        dve_emptied = sem("dve_emptied")
        act_emptied = sem("act_emptied")
        dve_chain = sem("dve_chain")
        pool_chain = sem("pool_chain")
        cond_in = sem("cond_in")
        wm_attn_in = [sem(f"wm_attn_in{c}") for c in range(IC)]
        wm_rest_in = sem("wm_rest_in")
        x_in = [sem(f"x_in{j}") for j in range(NB)]
        wq_in = sem("wq_in")
        wk_in = sem("wk_in")
        wv_in = sem("wv_in")
        b_col_in = sem("b_col_in")
        gate_in = sem("gate_in")
        kern_in = sem("kern_in")
        la_in = sem("la_in")
        lb_in = sem("lb_in")
        lsh_in = sem("lsh_in")
        bias_in = sem("bias_in")
        q_diag_in = sem("q_diag_in")
        v_diag_in = sem("v_diag_in")
        k_half_in = sem("k_half_in")
        b_tail_in = sem("b_tail_in")
        b_eff_in = [sem(f"b_eff_in{b}") for b in range(NB)]
        out_sent = sem("out_sent")
        ident_made = sem("ident_made")
        diag_zero = sem("diag_zero")
        k2_zero = sem("k2_zero")
        w_hi_made = sem("w_hi_made")
        h_hi_made = sem("h_hi_made")
        h_split = sem("h_split")
        h_split_end = sem("h_split_end")
        silu_ready = sem("silu_ready")
        mod_summed = sem("mod_summed")
        kern_hi_made = sem("kern_hi_made")
        kern_split = sem("kern_split")
        h2_begun = sem("h2_begun")
        h2_hi_made = sem("h2_hi_made")
        h2_split = sem("h2_split")
        bias_scaled = sem("bias_scaled")
        biased = sem("biased")
        ax_hi_made = sem("ax_hi_made")
        b_hi_made = sem("b_hi_made")
        b_split = sem("b_split")
        ga_ready = sem("ga_ready")
        gates_ready = sem("gates_ready")
        x_again = sem("x_again")
        exp_c = sem("exp_c")
        var_ready = sem("var_ready")
        std_ready = sem("std_ready")
        xn_ready = sem("xn_ready")
        shift_ready = sem("shift_ready")
        xn_by_act = sem("xn_by_act")
        shifted = sem("shifted")
        exped = sem("exped")
        inv_ready = sem("inv_ready")
        normed = sem("normed")
        turned = sem("turned")
        ctx_gated = sem("ctx_gated")
        ctx_low = sem("ctx_low")
        gmix_made = sem("gmix_made")
        masks_made = sem("masks_made")
        kern_scaled = sem("kern_scaled")
        tail_scaled = sem("tail_scaled")
        b_scaled = sem("b_scaled")
        ones_made = sem("ones_made")

        def bank(stage, i):
            b = use_no[stage, i] % BANKS
            return ps[:, b * BANK:(b + 1) * BANK]

        def written(stage, i):
            return use_no[stage, i] + 1

        def emptied(stage, i):
            u = use_no[stage, i]
            who = uses[u][2]
            return (dve_emptied if who == "v" else act_emptied), sum(1 for w in uses[:u + 1] if w[2] == who)

        block = ctx.enter_context(nc.Block())

        @block.sync
        def _(sp):
            sp.dma_start(silu[:, 0:IC], cond[0].rearrange("(c p) -> p c", p=P),
                         allow_slow_non_contiguous=True).then_inc(cond_in, 16)
            wm = wmod.rearrange("(c p) n -> p c n", p=P)
            xr = x[0].rearrange("(j p) n -> p j n", p=P)
            for j in range(NBH):
                sp.dma_start(xn_v[:, j, :], xr[:, j, :]).then_inc(x_in[j], 16)
            for c in range(IC):
                sp.dma_start(wm_attn[:, c, :], wm[:, c, 0:2 * hid]).then_inc(wm_attn_in[c], 16)
            for c in range(IC):
                sp.dma_start(wq_nat[:, c, :],
                             wq.rearrange("(h c d) n -> c d h n", c=IC, d=D)[c]).then_inc(wq_in, 16)
            for j in range(NBH, NB):
                sp.dma_start(xn_v[:, j, :], xr[:, j, :]).then_inc(x_in[j], 16)
            for c in range(IC):
                sp.dma_start(wk_nat[:, c, :],
                             wk.rearrange("(h c d) n -> c d h n", c=IC, d=D)[c]).then_inc(wk_in, 16)
            for n, bias_row in enumerate((bq, bk)):
                for c in range(IC):
                    sp.dma_start(b_col[:, n * IC + c:n * IC + c + 1],
                                 bias_row.rearrange("(h c d) -> c d h", c=IC, d=D)[c],
                                 allow_slow_non_contiguous=True).then_inc(b_col_in, 16)
            sp.dma_start(b_col[:, 2 * IC:3 * IC], bv.rearrange("(p c) -> p c", c=IC),
                         allow_slow_non_contiguous=True).then_inc(b_col_in, 16)
            sp.dma_start(wm_rest, wm[:, :, 2 * hid:6 * hid]).then_inc(wm_rest_in, 16)
            sp.dma_start(wv_nat, wv.rearrange("(p c) n -> p c n", c=IC)).then_inc(wv_in, 16)
            sp.dma_start(bs_nat, lora_bs.rearrange("(c p) r -> p c r", p=P)).then_inc(lsh_in, 16)
            for n in range(NG):
                for c in range(IC):
                    sp.dma_start(gate_col[rank * n:rank * (n + 1), c * NB:(c + 1) * NB],
                                 gate[:, NG * c + n].partition_broadcast(rank),
                                 allow_slow_non_contiguous=True).then_inc(gate_in, 16)
            sp.wait_ge(diag_zero, SLOT)
            for j in range(NB):
                if j % NBH == 0:
                    sp.wait_ge(*emptied("q", (j // NBH + 1) * IC - 1))
                sp.dma_start(diag_s[j * D:(j + 1) * D, j // HALF, :],
                             q_c[:, :, j * P:(j + 1) * P]).then_inc(q_diag_in, 16)
            sp.wait_ge(ga_ready, 1)
            sp.dma_start(as_nat[0:rank, :], lora_as[:, :]).then_inc(lsh_in, 16)
            sp.dma_start(bias_bc[:], bias.partition_broadcast(P)).then_inc(bias_in, 16)
            sp.wait_ge(k2_zero, HALF)
            for j in range(NB):
                if j % NBH == 0:
                    sp.wait_ge(*emptied("k", (j // NBH + 1) * IC - 1))
                sp.dma_start(k2_j[j * D:(j + 1) * D, j % HALF, :],
                             k_c[:, :, j * P:(j + 1) * P]).then_inc(k_half_in, 16)
            sp.wait_ge(psum_written, written("v", 2 * IC - 1))
            for c in range(IC):
                sp.dma_start(lb_nat[:, c, :].rearrange("p (n r) -> p n r", r=rank),
                             lora_b[:, c * P:(c + 1) * P, :].rearrange("n p r -> p n r")).then_inc(lb_in, 16)
            sp.dma_start(la_nat, lora_a.rearrange("(c n) r i -> (n r) c i", n=NG)).then_inc(la_in, 16)
            sp.wait_ge(psum_written, written("scores", NS - 1))
            sp.wait_ge(*emptied("v", 2 * IC - 1))
            for s in range(SLOT):
                for f in range(HALF):
                    j = HALF * s + f
                    sp.dma_start(diag_s[H * s:H * (s + 1), s, f * D * P:(f + 1) * D * P],
                                 v_c[:, :, j * P:(j + 1) * P]).then_inc(v_diag_in, 16)
            sp.wait_ge(v_diag_in, 16 * NB)
            sp.dma_start(xres.rearrange("p (j n) -> p j n", j=NB), xr).then_inc(x_again, 16)
            sp.wait_ge(turned, NCH)
            sp.dma_start(chunked(kern_nat), kern.rearrange("(c p) n -> p c n", p=P)).then_inc(kern_in, 16)
            sp.wait_ge(tail_scaled, 1)
            shared = slice(rank, 2 * rank)
            for r0 in (rank, 3 * rank):
                sp.dma_start(b_cat[r0:r0 + rank],
                             b_tail[shared, :].unsqueeze(1).to_broadcast([rank, NB, hid])).then_inc(b_tail_in, 16)
            for b in range(NB):
                q, r = b // NG, slice(rank * (b % NG), rank * (b % NG + 1))
                if b % NG == 0:
                    sp.wait_ge(b_scaled, q + 1)
                for r0 in (0, 2 * rank):
                    sp.dma_start(b_cat[r0:r0 + rank, b, :], b_raw[r, q, :]).then_inc(b_eff_in[b], 16)
            orow = out[0].rearrange("(j p) n -> p j n", p=P)
            for n, (j, cols) in enumerate(parts):
                sp.wait_ge(*emptied("out", n))
                sp.dma_start(orow[:, j, cols], x_v[:, j, cols]).then_inc(out_sent, 16)
            sp.wait_ge(out_sent, 16 * len(parts))

        @block.gpsimd
        def _(pool):
            nc.gpsimd.memset(ident[:], 0.0).then_inc(pool_chain, 1)
            pool.wait_ge(pool_chain, 1)
            nc.gpsimd.affine_select(out=ident[:], in_=ident[:], compare_op=ALU.not_equal, fill=1.0, base=0,
                                    pattern=[[-1, P]], channel_multiplier=1).then_inc(ident_made, 1)
            nc.gpsimd.memset(ones[:], 1.0).then_inc(ones_made, 1)

            def take_lo(banks):
                for i in banks:
                    k = i // IC
                    c = slice((i % IC) * tokens + k * BANK, (i % IC) * tokens + (k + 1) * BANK)
                    pool.wait_ge(h_hi_made, i + 1)
                    nc.gpsimd.tensor_tensor(hT_lo[:, c], h_full[:, i * BANK:(i + 1) * BANK], hT_hi[:, c].bitcast(F32),
                                            ALU.subtract).then_inc(h_split, 1)

            def clear(s):
                nc.gpsimd.memset(diag_s[:, s, :], 0.0).then_inc(diag_zero, 1)

            take_lo(range(IC))
            pool.wait_ge(psum_written, written("wq_t", IC - 1))
            clear(2)
            clear(3)
            take_lo(range(IC, IC + 2))
            pool.wait_ge(psum_written, written("h_t", 2 * IC - 1))
            clear(0)
            pool.wait_ge(h_split, IC + 2)
            pool.wait_ge(h_split_end, 2)
            clear(1)
            pool.wait_ge(gate_in, 16 * NG * IC)
            pool.wait_ge(masks_made, 1)
            nc.gpsimd.tensor_tensor(gmix.rearrange("p c (b r) -> p (c b) r", r=rank),
                                    gate_col[:].unsqueeze(2).to_broadcast([P, IC * NB, rank]),
                                    rank_mask[:].unsqueeze(1).to_broadcast([P, IC * NB, rank]),
                                    ALU.mult).then_inc(gmix_made, 1)
            pool.wait_ge(psum_written, written("wv_t", IC - 1))
            nc.gpsimd.memset(k2_j[:, 1, :], 0.0).then_inc(k2_zero, 1)
            pool.wait_ge(q_diag_in, 16 * NB)
            nc.gpsimd.memset(k2_j[:, 0, :], 0.0).then_inc(k2_zero, 1)
            for c in range(NCH):
                b = c % 2
                pool.wait_ge(inv_ready, c + 1)
                nc.gpsimd.tensor_tensor(s_rows[:, c], s_rows[:, c],
                                        rinv[:, b * RCH:(b + 1) * RCH].unsqueeze(2).to_broadcast([P, RCH, H]),
                                        ALU.mult).then_inc(normed, 1)
            pool.wait_ge(gates_ready, 1)
            pool.wait_ge(bias_in, 16)
            nc.gpsimd.tensor_tensor(bias_bc[:], bias_bc[:], gb_bc[:], ALU.mult).then_inc(bias_scaled, 1)
            pool.wait_ge(*emptied("bs_t", 0))
            pool.wait_ge(normed, NCH)
            pool.wait_ge(bias_scaled, 1)
            r = slice(rank, 2 * rank)
            nc.gpsimd.tensor_tensor(b_tail[r, :], b_tail[r, :], gb_bc[r, :], ALU.mult).then_inc(tail_scaled, 1)
            pool.wait_ge(tail_scaled, 1)
            s = 0
            while s < NS:
                if s == KERN_AT:
                    pool.wait_ge(kern_in, 16)
                    nc.gpsimd.tensor_tensor(chunked(kern_nat), chunked(kern_nat),
                                            gb_bc[:].unsqueeze(1).to_broadcast([P, IC, hid]),
                                            ALU.mult).then_inc(kern_scaled, 1)
                n = 2 if s < NS - 2 else 1
                pool.wait_ge(*emptied("ctx", s + n - 1))
                part = ctx_c[:, :, s * GB:(s + n) * GB]
                nc.gpsimd.tensor_tensor(part, part, ga_col[:].unsqueeze(2).to_broadcast([P, H, n * GB]),
                                        ALU.mult).then_inc(ctx_gated, 1)
                s += n

            def scale_b(i):
                pool.wait_ge(*emptied("b_eff", i))
                nc.gpsimd.tensor_tensor(b_raw[:, i, :], b_raw[:, i, :], gb_bc[:], ALU.mult).then_inc(b_scaled, 1)

            scale_b(0)
            for j in range(NB):
                if j == 1:
                    scale_b(1)
                pool.wait_ge(b_hi_made, j + 1)
                nc.gpsimd.tensor_tensor(b_lo[0:2 * rank, j, :], b_cat[0:2 * rank, j, :],
                                        b_hi[0:2 * rank, j, :].bitcast(F32), ALU.subtract).then_inc(b_split, 1)
                pool.wait_ge(xn_ready, XN_DVE + j + 1)
                nc.gpsimd.tensor_tensor(x_v[:, j, :], x_v[:, j, :], bias_bc[:], ALU.add).then_inc(biased, 1)

        @block.scalar
        def _(act):
            def empty(stage, i, dst, src=None):
                act.wait_ge(psum_written, written(stage, i))
                nc.scalar.activation(dst, bank(stage, i) if src is None else src, ACT.Copy).then_inc(act_emptied, 1)

            act.wait_ge(cond_in, 16)
            nc.scalar.activation(silu[:, IC:2 * IC], silu[:, 0:IC], ACT.Exp, scale=-1.0).then_inc(exp_c, 1)

            def take_hi(stage, i, hi):
                act.wait_ge(psum_written, written(stage, i))
                nc.scalar.activation(hi[:, i * BANK:(i + 1) * BANK], bank(stage, i), ACT.Copy).then_inc(w_hi_made, 1)

            def deviations(k, j0, j1):
                act.wait_ge(var_ready, k + 1)
                nc.scalar.activation(std[:, j0:j1], mv[:].rearrange("p (j s) -> p j s", s=2)[:, j0:j1, 1],
                                     ACT.Sqrt).then_inc(std_ready, 1)

            def h_t(i):
                act.wait_ge(psum_written, written("h_t", i))
                nc.scalar.activation(h_full[:, i * BANK:(i + 1) * BANK], bank("h_t", i), ACT.Identity,
                                     bias=modc[:, i % IC:i % IC + 1],
                                     scale=modc[:, IC + i % IC:IC + i % IC + 1]).then_inc(act_emptied, 1)

            def project(stage, i, dst, n):
                act.wait_ge(psum_written, written(stage, i))
                c = i % IC
                nc.scalar.activation(dst[:, c, (i // IC) * BANK:(i // IC + 1) * BANK], bank(stage, i), ACT.Identity,
                                     bias=b_col[:, n * IC + c:n * IC + c + 1]).then_inc(act_emptied, 1)

            deviations(0, 0, NBH)
            act.wait_ge(shift_ready, 1)
            for n, j in enumerate(XN_ACT):
                nc.scalar.activation(xn_v[:, j, :], xn_v[:, j, :], ACT.Identity, bias=shift[:, n:n + 1],
                                     scale=rstd[:, j:j + 1]).then_inc(xn_by_act, 1)
            for i in range(IC):
                act.wait_ge(*emptied("mod_attn", i // (IC // 2)))
                h_t(i)
                take_hi("wq_t", i, wA_hi)
            deviations(1, NBH, NB)
            for i in range(IC, 2 * IC):
                h_t(i)
            act.wait_ge(b_col_in, 16 * (2 * IC + 1))
            for i in range(IC):
                project("q", i, q_c, 0)
            for i in range(IC):
                take_hi("wk_t", i, wk_hi)
            for i in range(IC, 2 * IC):
                project("q", i, q_c, 0)
            for i in range(IC):
                take_hi("wv_t", i, wA_hi)
            act.wait_ge(mod_summed, 2)
            for i in range(2 * IC):
                project("k", i, k_c, 1)
            for i in range(V_FIRST):
                project("v", i, v_c, 2)

            def exp_chunk(c):
                act.wait_ge(shifted, c + 1)
                nc.scalar.activation(s_rows[:, c], s_rows[:, c], ACT.Exp, scale=SCALE).then_inc(exped, 1)

            act.wait_ge(k_half_in, 16 * NB)
            act.wait_ge(gates_ready, 1)
            for c in range(NCH):
                for s in (2 * c, 2 * c + 1):
                    empty("scores", s, sreg[:, s * BANK:(s + 1) * BANK])
                if c + V_FIRST < 2 * IC:
                    project("v", c + V_FIRST, v_c, 2)
                if c:
                    exp_chunk(c - 1)
            exp_chunk(NCH - 1)
            act.wait_ge(psum_written, written("as_t", 0))
            nc.scalar.activation(a_cat[:, :, :, rank:2 * rank],
                                 bank("as_t", 0)[:, 0:IC * rank].rearrange("p (c r) -> p c r", c=IC)
                                 .unsqueeze(2).to_broadcast([P, IC, NB, rank]), ACT.Copy).then_inc(act_emptied, 1)
            empty("bs_t", 0, b_tail[rank:2 * rank, :], bank("bs_t", 0)[0:rank, :])
            for i in range(IC):
                empty("b_t", i, b_t[:, i, :])

            def take_a_eff(i):
                empty("a_eff", i, a_cat[:, i, :, 0:rank],
                      bank("a_eff", i)[:, 0:NB * rank].rearrange("p (b r) -> p b r", b=NB))

            for i in range(IC - 1):
                take_a_eff(i)
            act.wait_ge(v_diag_in, 16 * NB)
            for s in range(NS):
                act.wait_ge(psum_written, written("ctx", s))
                nc.scalar.activation(ctx_w[:, s * GB:(s + 1) * GB, :],
                                     bank("ctx", s).rearrange("p (g f h) -> p g f h", f=HALF, h=H)[:, :, 0, :],
                                     ACT.Copy, scale=half_mask[:, 0:1]).then_inc(ctx_low, 1)
                if s == KERN_AT + 4:
                    act.wait_ge(kern_scaled, 1)
                    nc.scalar.activation(kern_hi, kern_nat, ACT.Copy).then_inc(kern_hi_made, 1)

            take_a_eff(IC - 1)

            def b_high_part(j):
                act.wait_ge(b_eff_in[j], 16 * 2)
                nc.scalar.activation(b_hi[:, j, :], b_cat[:, j, :], ACT.Copy).then_inc(b_hi_made, 1)

            def h2_t(j):
                act.wait_ge(psum_written, written("h2_t", j))
                for c in range(IC):
                    ins = nc.scalar.activation(h2F[:, j, c, :], bank("h2_t", j)[:, c * P:(c + 1) * P], ACT.Identity,
                                               bias=modc[:, 2 * IC + c:2 * IC + c + 1],
                                               scale=modc[:, 3 * IC + c:3 * IC + c + 1])
                    if j == 0 and c < IC - 1:
                        ins.then_inc(h2_begun, 1)
                ins.then_inc(act_emptied, 1)

            def h2_high_part(j):
                act.wait_ge(*emptied("h2_t", j))
                nc.scalar.activation(h2_hi[:, j * hid:(j + 1) * hid], h2_full[:, j * hid:(j + 1) * hid],
                                     ACT.Copy).then_inc(h2_hi_made, 1)

            deviations(2, 0, 2)
            empty("b_eff", 0, b_raw[:, 0, :])
            act.wait_ge(*emptied("mod_ffn", 0))
            h2_t(0)
            h2_high_part(0)
            act.wait_ge(b_tail_in, 16 * 2)
            deviations(3, 2, 4)
            h2_t(1)
            for j in range(NB):
                if 0 < j < NB - 1:
                    h2_t(j + 1)
                if j >= 2:
                    act.wait_ge(psum_written, written("out", j - 2))
                act.wait_ge(psum_written, written("ax", j))
                nc.scalar.activation(ax_parts[0:2 * rank, j % 2 * P:(j % 2 + 1) * P],
                                     bank("ax", j)[0:2 * rank, 0:P], ACT.Copy).then_inc(ax_hi_made, 1)
                if j == 0:
                    b_high_part(0)
                if j + 1 < NB:
                    h2_high_part(j + 1)
                if j == 0:
                    empty("b_eff", 1, b_raw[:, 1, :])
                if j + 1 < NB:
                    b_high_part(j + 1)
                if j % 2 == 0 and j + 4 < NB:
                    deviations(4 + j // 2, j + 4, j + 6)

        @block.vector
        def _(dve):
            chain = [0]

            def link(ins):
                chain[0] += 1
                ins.then_inc(dve_chain, 1)
                dve.wait_ge(dve_chain, chain[0])

            mv_v = mv[:].rearrange("p (j s) -> p j s", s=2)

            dve.wait_ge(exp_c, 1)
            link(nc.vector.tensor_scalar(silu[:, 2 * IC:3 * IC], silu[:, IC:2 * IC], 1.0, None, ALU.add))
            link(nc.vector.reciprocal(silu[:, 3 * IC:4 * IC], silu[:, 2 * IC:3 * IC]))
            nc.vector.tensor_tensor(silu[:, 2 * IC:3 * IC], silu[:, 0:IC], silu[:, 3 * IC:4 * IC],
                                    ALU.mult).then_inc(silu_ready, 1)

            def layer_norm_stats(j0, j1, x_v, arrived=None):
                for j in range(j0, j1):
                    if arrived:
                        dve.wait_ge(arrived[j], 16)
                    ins = nc.vector.bn_stats(stats[:, 6 * j:6 * j + 6], x_v[:, j, :])
                link(ins)
                for j in range(j0, j1):
                    ins = nc.vector.bn_aggr(mv_v[:, j, :], stats[:, 6 * j:6 * j + 6])
                link(ins)
                nc.vector.tensor_scalar(mv_v[:, j0:j1, 1], mv_v[:, j0:j1, 1], EPS, None, ALU.add).then_inc(var_ready, 1)

            def normalise(k, j0, j1, dst, x_v, by_act=range(0)):
                dve.wait_ge(std_ready, k + 1)
                link(nc.vector.reciprocal(rstd[:, j0:j1], std[:, j0:j1]))
                if by_act:
                    a = slice(by_act[0], by_act[-1] + 1)
                    nc.vector.scalar_tensor_tensor(out=shift[:], in0=mv_v[:, a, 0], scalar=-1.0, in1=rstd[:, a],
                                                   op0=ALU.mult, op1=ALU.mult).then_inc(shift_ready, 1)
                for j in range(j0, j1):
                    if j in by_act:
                        continue
                    nc.vector.tensor_scalar(dst[:, j, :], x_v[:, j, :], mv_v[:, j, 0:1], rstd[:, j:j + 1],
                                            ALU.subtract, ALU.mult).then_inc(xn_ready, 1)

            def modulation(w, arrived):
                dve.wait_ge(silu_ready, 1)
                dve.wait_ge(arrived[0], 16)
                link(nc.vector.tensor_scalar(w[:, 0], w[:, 0], silu[:, 2 * IC:2 * IC + 1], None, ALU.mult))
                for c in range(1, IC):
                    dve.wait_ge(arrived[c], 16)
                    ins = nc.vector.scalar_tensor_tensor(out=w[:, 0], in0=w[:, c],
                                                         scalar=silu[:, 2 * IC + c:2 * IC + c + 1], in1=w[:, 0],
                                                         op0=ALU.mult, op1=ALU.add)
                    if c + 1 < IC:
                        link(ins)
                ins.then_inc(mod_summed, 1)

            def mod_columns(stage, i, o0, n):
                dve.wait_ge(psum_written, written(stage, i))
                nc.vector.tensor_copy(modc[:, o0:o0 + n], bank(stage, i)[:, 0:n])
                nc.vector.tensor_scalar(modc[:, o0 + IC:o0 + IC + n], bank(stage, i)[:, n:2 * n], 1.0, None,
                                        ALU.add).then_inc(dve_emptied, 1)

            weights_taken = [0]

            def take_lo(stage, i, hi, lo):
                weights_taken[0] += 1
                dve.wait_ge(w_hi_made, weights_taken[0])
                c = slice(i * BANK, (i + 1) * BANK)
                nc.vector.tensor_tensor(lo[:, c], bank(stage, i), hi[:, c].bitcast(F32),
                                        ALU.subtract).then_inc(dve_emptied, 1)

            def take_h_hi(i):
                c = slice((i % IC) * tokens + i // IC * BANK, (i % IC) * tokens + (i // IC + 1) * BANK)
                dve.wait_ge(*emptied("h_t", i))
                nc.vector.tensor_copy(hT_hi[:, c], h_full[:, i * BANK:(i + 1) * BANK]).then_inc(h_hi_made, 1)

            layer_norm_stats(0, NBH, xn_v, x_in)
            normalise(0, 0, NBH, xn_v, xn_v, XN_ACT)
            modulation(wm_attn, wm_attn_in)
            dve.wait_ge(ident_made, 1)
            nc.vector.tensor_reduce(half_mask[:], ident[:].rearrange("p (s f d) -> p f s d", f=HALF, d=D), AX_XY, ALU.add)
            nc.vector.tensor_reduce(d_mask[:], ident[:].rearrange("p (j d) -> p d j", d=D), AX_X, ALU.add)
            nc.vector.tensor_reduce(rank_mask[:], ident[:].rearrange("p (n r) -> p r n", r=rank), AX_X,
                                    ALU.add).then_inc(masks_made, 1)
            mod_columns("mod_attn", 0, 0, IC // 2)
            mod_columns("mod_attn", 1, IC // 2, IC // 2)
            for i in range(IC):
                take_h_hi(i)
                take_lo("wq_t", i, wA_hi, wA_lo)
            layer_norm_stats(NBH, NB, xn_v, x_in)
            normalise(1, NBH, NB, xn_v, xn_v)
            for i in range(IC, 2 * IC):
                take_h_hi(i)
            for i in range(IC + 2, 2 * IC):
                c = slice(i % IC * tokens + BANK, i % IC * tokens + 2 * BANK)
                dve.wait_ge(h_hi_made, i + 1)
                nc.vector.tensor_tensor(hT_lo[:, c], h_full[:, i * BANK:(i + 1) * BANK], hT_hi[:, c].bitcast(F32),
                                        ALU.subtract).then_inc(h_split_end, 1)
            for i in range(IC):
                take_lo("wk_t", i, wk_hi, wk_lo)
            modulation(wm_rest, [wm_rest_in] * IC)
            for i in range(IC):
                take_lo("wv_t", i, wA_hi, wA_lo)
            mod_columns("mod_ffn", 0, 2 * IC, IC)
            dve.wait_ge(masks_made, 1)
            for name, dst in (("gate_attn", ga_bc), ("gate_ffn", gb_bc)):
                dve.wait_ge(psum_written, written(name, 0))
                link(nc.vector.tensor_scalar(sign_tmp, bank(name, 0), 0.0, 2.0, ALU.is_ge, ALU.mult))
                nc.vector.scalar_tensor_tensor(out=dst[:], in0=sign_tmp, scalar=-1.0, in1=bank(name, 0),
                                               op0=ALU.add, op1=ALU.mult).then_inc(dve_emptied, 1)
                dve.wait_ge(*emptied(name, 0))
                link(nc.vector.tensor_scalar(dst[:], dst[:], GATE_FLOOR, None, ALU.max))
                ins = nc.vector.scalar_tensor_tensor(out=dst[:], in0=sign_tmp, scalar=-1.0, in1=dst[:],
                                                     op0=ALU.add, op1=ALU.mult)
                if name == "gate_attn":
                    link(ins)
                    link(nc.vector.tensor_tensor(sign_tmp.rearrange("p (h d) -> p h d", d=D),
                                                 ga_bc[:].rearrange("p (h d) -> p h d", d=D),
                                                 d_mask[:].unsqueeze(1).to_broadcast([P, H, D]), ALU.mult))
                    ins = nc.vector.tensor_reduce(ga_col[:], sign_tmp.rearrange("p (h d) -> p h d", d=D), AX_X,
                                                  ALU.add)
                    ins.then_inc(ga_ready, 1)
                    dve.wait_ge(ga_ready, 1)
                else:
                    ins.then_inc(gates_ready, 1)

            def row_max(c):
                b = c % 2
                dve.wait_ge(*emptied("scores", 2 * c + 1))
                m = rmax[:, b * RCH:(b + 1) * RCH]
                link(nc.vector.tensor_reduce(m, s_rows[:, c], AX_X, ALU.max))
                nc.vector.tensor_tensor(s_rows[:, c], s_rows[:, c], m.unsqueeze(2).to_broadcast([P, RCH, H]),
                                        ALU.subtract).then_inc(shifted, 1)

            def row_sum(c):
                b = c % 2
                dve.wait_ge(exped, c + 1)
                link(nc.vector.tensor_reduce(rsum[:, b * RCH:(b + 1) * RCH], s_rows[:, c], AX_X, ALU.add))
                if c >= 2:
                    dve.wait_ge(normed, c - 1)
                nc.vector.reciprocal(rinv[:, b * RCH:(b + 1) * RCH], rsum[:, b * RCH:(b + 1) * RCH]).then_inc(inv_ready, 1)

            for c in range(NCH):
                row_max(c)
                if c:
                    row_sum(c - 1)

            def turn(c):
                dve.wait_ge(normed, c + 1)
                nc.vector.transpose(p_t[:, c * CH:(c + 1) * CH], sreg[:, c * CH:(c + 1) * CH]).then_inc(turned, 1)

            dve.wait_ge(psum_written, written("scores", NS - 1))
            turn(0)
            row_sum(NCH - 1)
            for c in range(1, NCH):
                turn(c)
            for s in range(NS):
                dve.wait_ge(ctx_low, s + 1)
                dst = ctx_w[:, s * GB:(s + 1) * GB, :]
                nc.vector.scalar_tensor_tensor(
                    out=dst, in0=bank("ctx", s).rearrange("p (g f h) -> p g f h", f=HALF, h=H)[:, :, 1, :],
                    scalar=half_mask[:, 1:2], in1=dst, op0=ALU.mult, op1=ALU.add).then_inc(dve_emptied, 1)
                if s == KERN_AT + 4:
                    dve.wait_ge(kern_hi_made, 1)
                    nc.vector.tensor_tensor(kern_lo, kern_nat, kern_hi.bitcast(F32),
                                            ALU.subtract).then_inc(kern_split, 1)
            dve.wait_ge(x_again, 16)
            for i in range(NHG):
                dve.wait_ge(psum_written, written("ctx_t", i))
                dst = x_hjd[:, 4 * i:4 * i + 4]
                nc.vector.tensor_tensor(dst, bank("ctx_t", i).rearrange("p (h j d) -> p h j d", h=4, d=D), dst,
                                        ALU.add).then_inc(dve_emptied, 1)
            dve.wait_ge(*emptied("ctx_t", NHG - 1))

            def split_h2(j):
                c = slice(j * hid, (j + 1) * hid)
                dve.wait_ge(h2_hi_made, j + 1)
                nc.vector.tensor_tensor(h2_lo[:, c], h2_full[:, c], h2_hi[:, c].bitcast(F32),
                                        ALU.subtract).then_inc(h2_split, 1)

            layer_norm_stats(0, 2, x_v)
            normalise(2, 0, 2, xn2, x_v)
            layer_norm_stats(2, 4, x_v)
            split_h2(0)
            normalise(3, 2, 4, xn2, x_v)
            for j in range(NB):
                dve.wait_ge(ax_hi_made, j + 1)
                c = slice(j % 2 * P, (j % 2 + 1) * P)
                nc.vector.tensor_tensor(ax_parts[2 * rank:4 * rank, c], bank("ax", j)[0:2 * rank, 0:P],
                                        ax_parts[0:2 * rank, c].bitcast(F32), ALU.subtract).then_inc(dve_emptied, 1)
                if j < NB - 1:
                    split_h2(j + 1)
                if j % 2 == 0 and j + 4 < NB:
                    layer_norm_stats(j + 4, j + 6, x_v)
                if j % 2 == 1 and j + 3 < NB:
                    normalise(4 + j // 2, j + 3, j + 5, xn2, x_v)
                dve.wait_ge(biased, j + 1)
                for n, (_, cols) in enumerate(parts):
                    if parts[n][0] == j:
                        dve.wait_ge(psum_written, written("out", n))
                        nc.vector.tensor_tensor(x_v[:, j, cols], bank("out", n)[:, 0:cols.stop - cols.start],
                                                x_v[:, j, cols], ALU.add).then_inc(dve_emptied, 1)

        @block.tensor
        def _(pe):
            def take(stage, i):
                u = use_no[stage, i]
                if u >= BANKS:
                    pe.wait_ge(*emptied(*uses[u - BANKS][0:2]))
                return bank(stage, i)

            def mod_columns(stage, i, w, cols):
                dst = take(stage, i)
                for n, o0 in enumerate(cols):
                    ins = nc.tensor.matmul(dst[:, n:n + 1], w[:, 0, o0:o0 + P], ones[:, 0:1], start=True, stop=True)
                ins.then_inc(psum_written, 1)

            def gate_rows(stage, o0):
                nc.tensor.matmul(take(stage, 0), ones[:], wm_rest[:, 0, o0:o0 + hid],
                                 start=True, stop=True).then_inc(psum_written, 1)

            def transposes(stage, i, blocks):
                dst = take(stage, i)
                for n, src in enumerate(blocks):
                    k, m = src.shape[0], src.shape[1]
                    ins = nc.tensor.transpose(dst[0:m, n * k:(n + 1) * k], src, ident[0:k, 0:k])
                ins.then_inc(psum_written, 1)

            def weight_t(stage, w_nat, chunks):
                for i in chunks:
                    transposes(stage, i, [w_nat[:, c, i * P:(i + 1) * P] for c in range(IC)])

            def split_product(dst, a_hi, a_lo, b_hi, b_lo, start, stop):
                nc.tensor.matmul(dst, a_hi, b_lo, start=start, stop=False)
                nc.tensor.matmul(dst, a_lo, b_hi, start=False, stop=False)
                return nc.tensor.matmul(dst, a_hi, b_hi, start=False, stop=stop)

            def project_part(dst, k, o, c, w_hi, w_lo):
                t = slice(c * tokens + k * BANK, c * tokens + (k + 1) * BANK)
                w = slice(c * hid + o * P, c * hid + (o + 1) * P)
                return split_product(dst, w_hi[:, w], w_lo[:, w], hT_hi[:, t], hT_lo[:, t], c == 0, c == IC - 1)

            def project(stage, i, w_hi, w_lo):
                dst = take(stage, i)
                for c in range(IC):
                    ins = project_part(dst, i // IC, i % IC, c, w_hi, w_lo)
                ins.then_inc(psum_written, 1)

            def h_t(k):
                pe.wait_ge(xn_ready, (k + 1) * NBH - len(XN_ACT))
                pe.wait_ge(xn_by_act, len(XN_ACT))
                for i in range(IC):
                    transposes("h_t", k * IC + i,
                               [xn_v[:, j, i * P:(i + 1) * P] for j in range(k * NBH, (k + 1) * NBH)])

            pe.wait_ge(ident_made, 1)
            h_t(0)
            pe.wait_ge(ones_made, 1)
            pe.wait_ge(mod_summed, 1)
            for i in range(2):
                mod_columns("mod_attn", i, wm_attn,
                            [(k * IC + i * IC // 2 + c) * P for k in range(2) for c in range(IC // 2)])
            pe.wait_ge(wq_in, 16 * IC)
            weight_t("wq_t", wq_nat, range(IC))
            for c in range(IC):
                pe.wait_ge(h_split, c + 1)
                pe.wait_ge(*emptied("wq_t", c))
                for o in range(IC):
                    ins = project_part(take("q", o) if c == 0 else bank("q", o), 0, o, c, wA_hi, wA_lo)
                    if c == IC - 1:
                        ins.then_inc(psum_written, 1)
                if c == IC - 2:
                    h_t(1)
            pe.wait_ge(wk_in, 16 * IC)
            weight_t("wk_t", wk_nat, range(IC))
            pe.wait_ge(h_split, IC + 2)
            pe.wait_ge(h_split_end, 2)
            for i in range(IC, 2 * IC):
                project("q", i, wA_hi, wA_lo)
            pe.wait_ge(wv_in, 16)
            weight_t("wv_t", wv_nat, range(IC))
            pe.wait_ge(*emptied("wk_t", IC - 1))
            for i in range(2):
                project("k", i, wk_hi, wk_lo)
            pe.wait_ge(mod_summed, 2)
            mod_columns("mod_ffn", 0, wm_rest, [hid + c * P for c in range(2 * IC)])
            gate_rows("gate_attn", 0)
            gate_rows("gate_ffn", 3 * hid)
            for i in range(2, 2 * IC):
                project("k", i, wk_hi, wk_lo)
            pe.wait_ge(*emptied("wv_t", IC - 1))
            for i in range(V_FIRST):
                project("v", i, wA_hi, wA_lo)
            pe.wait_ge(q_diag_in, 16 * NB)
            pe.wait_ge(k_half_in, 16 * NB)
            for s in range(NS):
                dst = take("scores", s)
                for n in range(GB):
                    g = s * GB + n
                    ins = nc.tensor.matmul(dst[:, n * HALF * H:(n + 1) * HALF * H], diag_g[:, :, g], k2_g[:, :, g],
                                           start=True, stop=True)
                ins.then_inc(psum_written, 1)
                if s % 2 and s // 2 + V_FIRST < 2 * IC:
                    project("v", s // 2 + V_FIRST, wA_hi, wA_lo)

            pe.wait_ge(lsh_in, 32)
            transposes("as_t", 0, [as_nat[0:rank, c * P:(c + 1) * P] for c in range(IC)])
            transposes("bs_t", 0, [bs_nat[:, c, :] for c in range(IC)])
            pe.wait_ge(lb_in, 16 * IC)
            weight_t("b_t", lb_nat, range(IC))
            pe.wait_ge(la_in, 16)
            pe.wait_ge(gmix_made, 1)

            def a_eff(i):
                dst = take("a_eff", i)
                for c in range(IC):
                    ins = nc.tensor.matmul(dst[:, 0:NB * rank], la_nat[:, c, i * P:(i + 1) * P], gmix[:, c, :],
                                           start=(c == 0), stop=(c == IC - 1))
                ins.then_inc(psum_written, 1)

            for i in range(IC - 1):
                a_eff(i)

            def b_eff(i, chunks):
                for c in chunks:
                    dst = take("b_eff", i) if c == 0 else bank("b_eff", i)
                    ins = nc.tensor.matmul(dst, gmix[:, c, i * P:(i + 1) * P], b_t[:, c, :],
                                           start=(c == 0), stop=(c == IC - 1))
                    if c == IC - 1:
                        ins.then_inc(psum_written, 1)

            pe.wait_ge(v_diag_in, 16 * NB)
            for s in range(NS):
                if s % 2 == 0:
                    pe.wait_ge(turned, s // 2 + 1)
                dst = take("ctx", s)
                for n in range(GB):
                    g = s * GB + n
                    ins = nc.tensor.matmul(dst[:, n * HALF * H:(n + 1) * HALF * H], diag_g[:, :, g], pT_g[:, g, :],
                                           start=True, stop=True)
                ins.then_inc(psum_written, 1)
            a_eff(IC - 1)
            pe.wait_ge(ctx_gated, NS // 2 + 1)
            for i in range(NHG):
                transposes("ctx_t", i, [ctx_c[:, h, :] for h in range(4 * i, 4 * i + 4)])

            def h2_t(j):
                pe.wait_ge(xn_ready, XN_DVE + j + 1)
                transposes("h2_t", j, [xn2[:, j, c * P:(c + 1) * P] for c in range(IC)])

            def out_part(n, j, cols):
                dst = take("out", n)[:, 0:cols.stop - cols.start]
                for c in range(IC):
                    t, o = slice(j * hid + c * P, j * hid + (c + 1) * P), slice(c * hid + cols.start, c * hid + cols.stop)
                    split_product(dst, h2_hi[:, t], h2_lo[:, t], kern_hi[:, o], kern_lo[:, o], c == 0, False)
                pe.wait_ge(b_split, j + 1)
                pe.wait_ge(*emptied("ax", j))
                t = slice(j % 2 * P, (j % 2 + 1) * P)
                nc.tensor.matmul(dst, ax_parts[:, t], b_hi[:, j, cols], start=False, stop=False)
                nc.tensor.matmul(dst, ax_parts[0:2 * rank, t], b_lo[0:2 * rank, j, cols],
                                 start=False, stop=True).then_inc(psum_written, 1)

            pe.wait_ge(*emptied("b_t", IC - 1))
            b_eff(0, range(IC))
            b_eff(1, [0, 1])
            h2_t(0)
            h2_t(1)
            b_eff(1, [2])
            for j in range(NB):
                if 0 < j < NB - 1:
                    h2_t(j + 1)
                if j == 0:
                    pe.wait_ge(*emptied("a_eff", IC - 1))
                dst = take("ax", j)[0:2 * rank, 0:P]
                for c in range(IC):
                    if j == 0 and c < IC - 1:
                        pe.wait_ge(h2_begun, c + 1)
                    elif c == IC - 1 or c == 0:
                        pe.wait_ge(*emptied("h2_t", j))
                    ins = nc.tensor.matmul(dst, a_cat[:, c, j, :], h2F[:, j, c, :], start=(c == 0), stop=(c == IC - 1))
                ins.then_inc(psum_written, 1)
                if j == 0:
                    b_eff(1, [3])
                    pe.wait_ge(kern_split, 1)
                pe.wait_ge(h2_split, j + 1)
                for n, (_, cols) in enumerate(parts):
                    if parts[n][0] == j:
                        out_part(n, j, cols)


_INS = ["L0_attn_hidden_states", "L0_attn_wq", "L0_attn_bq", "L0_attn_wk", "L0_attn_bk", "L0_attn_wv", "L0_attn_bv",
        "L0_ffn_gate", "L0_ffn_kernel", "L0_ffn_bias", "L0_ffn_lora_A", "L0_ffn_lora_B", "L0_ffn_lora_A_shared",
        "L0_ffn_lora_B_shared", "L0_c", "L0_wmod"]
_OUTS = [((1, 1024, 512), "float32")]


def kernel(**inputs):
    import numpy as _np
    import concourse.bacc as _bacc
    from concourse import mybir as _mybir
    from concourse.bass_utils import run_bass_kernel_spmd as _run

    nc = _bacc.Bacc("TRN2", target_bir_lowering=False, num_devices=1)
    arrays, args = {}, []
    for name in _INS:
        a = _np.ascontiguousarray(inputs[name])
        arrays[f"in_{name}_dram"] = a
        args.append(nc.dram_tensor(f"in_{name}_dram", a.shape, _mybir.dt.from_np(a.dtype), kind="ExternalInput").ap())
    for i, (shape, dtype) in enumerate(_OUTS):
        dt = _mybir.dt.from_np(_np.dtype(dtype))
        args.append(nc.dram_tensor(f"out_{i}_dram", shape, dt, kind="ExternalOutput").ap())
    adaln_block(nc, *args)
    r = _run(nc, [arrays], core_ids=[0])
    return r.results[0]["out_0_dram"]
```
